# Optimizing a Trainium2 kernel written in Bass

```python
import numpy as np
import jax
import jax.numpy as jnp

def _softmax(x, axis=-1):
    return jax.nn.softmax(x, axis=axis)

def _gelu(x):
    return jax.nn.gelu(x, approximate=True)

def _silu(x):
    return jax.nn.silu(x)

def _sigmoid(x):
    return jax.nn.sigmoid(x)

def _layernorm(x, axis=-1, eps=1e-05):
    m = jnp.mean(x, axis=axis, keepdims=True)
    v = jnp.var(x, axis=axis, keepdims=True)
    return (x - m) / jnp.sqrt(v + eps)

def _scatter_add(tgt, idx, src, axis=0):
    return tgt.at[idx].add(src)

def _segment_sum(src, seg, n):
    return jax.ops.segment_sum(src, seg, n)
kernel_name = 'mk_prb_d1_jaxref_r4_a5697a'

def setup_inputs(seed: int=0):
    np.random.seed(seed)
    _w = jnp.asarray

    def _L0_attn_setup():
        import jax, jax.numpy as jnp
        import numpy as np
        DIM = 256
        B, N = (8, 1024)
        EPS = 1e-06
        key = jax.random.key(seed)
        k1, k2, k3, k4 = jax.random.split(key, 4)
        x = jax.random.normal(k1, (B, N, DIM), dtype=jnp.float32)
        s = 1.0 / np.sqrt(DIM)
        W_qkv = jax.random.uniform(k2, (3 * DIM, DIM), jnp.float32, -s, s)
        W_out = jax.random.uniform(k3, (DIM, DIM), jnp.float32, -s, s)
        b_out = jax.random.uniform(k4, (DIM,), jnp.float32, -s, s)
        return {'x': x, 'W_qkv': W_qkv, 'W_out': W_out, 'b_out': b_out}
    _L0_attn_in = _L0_attn_setup()

    def _L0_ffn_setup():
        import jax, jax.numpy as jnp
        import numpy as np
        B, T, C = (2, 128, 256)
        I = 1024
        E = 8
        K = 2
        key = jax.random.key(seed)
        ks = jax.random.split(key, 8)
        s = 0.02
        return {'x': jax.random.normal(ks[0], (B, T, C), jnp.float32), 'Wr1': jax.random.normal(ks[1], (C, C // 4), jnp.float32) * s, 'br1': jnp.zeros((C // 4,), jnp.float32), 'Wr2': jax.random.normal(ks[2], (C // 4, E), jnp.float32) * s, 'br2': jnp.zeros((E,), jnp.float32), 'Ws1': jax.random.normal(ks[3], (C, I), jnp.float32) * s, 'bs1': jnp.zeros((I,), jnp.float32), 'Ws2': jax.random.normal(ks[4], (I, C), jnp.float32) * s, 'bs2': jnp.zeros((C,), jnp.float32), 'We1': jax.random.normal(ks[5], (E, C, I), jnp.float32) * s, 'be1': jnp.zeros((E, I), jnp.float32), 'We2': jax.random.normal(ks[6], (E, I, C), jnp.float32) * s, 'be2': jnp.zeros((E, C), jnp.float32)}
    _L0_ffn_in = _L0_ffn_setup()
    _d = {'L0_attn_x': _L0_attn_in['x'], 'L0_attn_W_qkv': _L0_attn_in['W_qkv'], 'L0_attn_W_out': _L0_attn_in['W_out'], 'L0_attn_b_out': _L0_attn_in['b_out'], 'L0_ffn_Wr1': _L0_ffn_in['Wr1'], 'L0_ffn_br1': _L0_ffn_in['br1'], 'L0_ffn_Wr2': _L0_ffn_in['Wr2'], 'L0_ffn_br2': _L0_ffn_in['br2'], 'L0_ffn_Ws1': _L0_ffn_in['Ws1'], 'L0_ffn_bs1': _L0_ffn_in['bs1'], 'L0_ffn_Ws2': _L0_ffn_in['Ws2'], 'L0_ffn_bs2': _L0_ffn_in['bs2'], 'L0_ffn_We1': _L0_ffn_in['We1'], 'L0_ffn_be1': _L0_ffn_in['be1'], 'L0_ffn_We2': _L0_ffn_in['We2'], 'L0_ffn_be2': _L0_ffn_in['be2']}
    _x0 = _d['L0_attn_x']
    _d['L0_attn_x'] = jax.random.normal(jax.random.fold_in(jax.random.key(seed), 1), (8, 512, 256), dtype=_x0.dtype)
    del _x0
    return _d

def reference(L0_attn_x, L0_attn_W_qkv, L0_attn_W_out, L0_attn_b_out, L0_ffn_Wr1, L0_ffn_br1, L0_ffn_Wr2, L0_ffn_br2, L0_ffn_Ws1, L0_ffn_bs1, L0_ffn_Ws2, L0_ffn_bs2, L0_ffn_We1, L0_ffn_be1, L0_ffn_We2, L0_ffn_be2):

    def _L0_attn_ref(x, W_qkv, W_out, b_out):
        import jax, jax.numpy as jnp
        import numpy as np
        DIM = 256
        B, N = (8, 1024)
        EPS = 1e-06
        qkv = jnp.einsum('bnd,ed->bne', x, W_qkv)
        q, k, v = jnp.split(qkv, 3, axis=-1)
        q = jax.nn.relu(q) + EPS
        k = jax.nn.relu(k) + EPS
        kv = jnp.einsum('bnd,bne->bde', k, v)
        z = 1.0 / (jnp.einsum('bnd,bd->bn', q, k.sum(axis=1)) + EPS)
        attn = jnp.einsum('bnd,bde,bn->bne', q, kv, z)
        return jnp.einsum('bne,fe->bnf', attn, W_out) + b_out

    def _L0_ffn_ref(x, Wr1, br1, Wr2, br2, Ws1, bs1, Ws2, bs2, We1, be1, We2, be2):
        import jax, jax.numpy as jnp
        import numpy as np
        B, T, C = (2, 128, 256)
        I = 1024
        E = 8
        K = 2
        Bb, Tt, Cc = x.shape
        xf = x.reshape(-1, Cc)
        logits = jax.nn.relu(xf @ Wr1 + br1) @ Wr2 + br2
        gates = jax.nn.softmax(logits, axis=-1)
        tg, ti = jax.lax.top_k(gates, K)
        tg = jax.nn.softmax(tg / K, axis=-1)
        out = jax.nn.silu(xf @ Ws1 + bs1) @ Ws2 + bs2
        for e in range(E):
            h = jax.nn.silu(xf @ We1[e] + be1[e]) @ We2[e] + be2[e]
            w = jnp.sum(tg * (ti == e), axis=-1)
            out = out + w[:, None] * h
        return out.reshape(Bb, Tt, Cc)
    x = L0_attn_x
    xn = _layernorm(x, axis=-1)
    x = x + _L0_attn_ref(xn, L0_attn_W_qkv, L0_attn_W_out, L0_attn_b_out) + _L0_ffn_ref(xn, L0_ffn_Wr1, L0_ffn_br1, L0_ffn_Wr2, L0_ffn_br2, L0_ffn_Ws1, L0_ffn_bs1, L0_ffn_Ws2, L0_ffn_bs2, L0_ffn_We1, L0_ffn_be1, L0_ffn_We2, L0_ffn_be2)
    return x

_drawn_inputs = setup_inputs


def setup_inputs(seed=0):
    import zlib

    import numpy as np

    out = dict(_drawn_inputs(seed))
    spreads = {'L0_ffn_br1': (0.0, 0.1),
     'L0_ffn_br2': (0.0, 0.1),
     'L0_ffn_bs1': (0.0, 0.1),
     'L0_ffn_bs2': (0.0, 0.1),
     'L0_ffn_be1': (0.0, 0.35),
     'L0_ffn_be2': (0.0, 0.1)}
    factors = {'L0_attn_W_qkv': 3.697, 'L0_attn_W_out': 3.624}
    for name, (base, spread) in spreads.items():
        noise = np.random.default_rng([zlib.crc32(name.encode()), seed]).standard_normal(out[name].shape)
        drawn = base * np.exp(spread * noise) if base else spread * noise
        out[name] = jnp.asarray(drawn.astype(out[name].dtype))
    for name, factor in factors.items():
        out[name] = (out[name] * factor).astype(out[name].dtype)
    return out
```

```python
import concourse.bass as bass
from concourse import mybir
from contextlib import ExitStack

P = 128
ROWS, C, I, E = 4096, 256, 1024, 8
NB, SEQ = 8, 512
TB = SEQ // P
NG = ROWS // P
HID = C // 4
TILE = 256
NT = (2 * ROWS + E * (TILE - 1)) // TILE
NS = ROWS // TILE
NALL = NT + NS
COLS = NT * 2
CHUNK = 1024
CE = 4
S_X, S_W, S_Q, S_KV, S_H = 256.0, 256.0, 64.0, 0.125, 64.0
LN_EPS, EPS = 1e-5, 1e-6
XT0 = (E - 1) * CE


def build_program(nc, x, wts, wa, wr, br1, wr2, br2, b1, b2, bo, out):
    f32, f16, i32 = mybir.dt.float32, mybir.dt.float16, mybir.dt.int32
    ALU, ACT, AX = mybir.AluOpType, mybir.ActivationFunctionType, mybir.AxisListType
    ds = bass.ds

    rows_d = nc.dram_tensor("rows_scratch", (ROWS, 2 * C), f16).ap()
    base_d = nc.dram_tensor("base_scratch", (ROWS, C), f32).ap()
    ys_d = nc.dram_tensor("expert_out_scratch", (NT * TILE, C), f32).ap()
    x_v = x.rearrange("(b p t) c -> b p (t c)", b=NB, t=TB)
    base_v = base_d.rearrange("(b p t) c -> b p (t c)", b=NB, t=TB)
    rows_v = rows_d.rearrange("(b p t) c -> b p (t c)", b=NB, t=TB)
    rows_s = rows_d.rearrange("(b p u h) c -> u b p (h c)", b=NB, u=2, h=2)
    base_s = base_d.rearrange("(b p u h) c -> u b p (h c)", b=NB, u=2, h=2)
    out_s = out.rearrange("(b p u h) c -> u b p (h c)", b=NB, u=2, h=2)
    ys_v = ys_d.rearrange("(j p h) c -> j p (h c)", p=P, h=2)

    ctx = ExitStack()
    with ctx:
        def sem(name):
            return ctx.enter_context(nc.semaphore(name))

        def sem2(name):
            return [sem(name + "_even"), sem(name + "_odd")]

        def sb(stack, name, shape, dt):
            return stack.enter_context(nc.sbuf_tensor(name, shape, dt))

        Wt = sb(ctx, "expert_weights", [P, (E + 1) * CE, 2, CHUNK], f16)
        stage = sb(ctx, "weight_stage", [P, 2, CHUNK], f32)
        xs = sb(ctx, "x_rows", [P, 2, TB * C], f32)
        list_i = sb(ctx, "list_rows", [P, COLS], i32)
        pos_i = sb(ctx, "places", [P, NG * 2], i32)
        wc = sb(ctx, "gate_weights", [P, NG, 2], f32)
        et = sb(ctx, "tile_experts", [1, 3, NALL + 1], i32)
        b1s = sb(ctx, "b1_columns", [P, (E + 1) * 8], f32)

        pa = ExitStack()
        Wa = sb(pa, "attention_weights", [P, 2, 2, CHUNK], f16)
        Wrf = sb(pa, "router_w1_f32", [P, 2, HID], f32)
        Wr = sb(pa, "router_w1", [P, 2, 2, HID], f16)
        wr2s = sb(pa, "router_w2", [HID, E], f32)
        br1s = sb(pa, "router_b1", [HID, 1], f32)
        br2s = sb(pa, "router_b2", [P, E], f32)
        ident = sb(pa, "ident", [P, P], f16)
        before = sb(pa, "before", [P, P], f16)
        ones = sb(pa, "ones", [P, P], f16)
        half = sb(pa, "half", [P, 1], f16)
        iota_p = sb(pa, "iota_partition", [P, P], f16)
        iota_c = sb(pa, "iota_column", [P, COLS], f16)
        tok_l = sb(pa, "row_in_batch", [P, TB], f32)
        tok_b = sb(pa, "batch_rows", [P, NB], f32)
        list_f = sb(pa, "list_f32", [P, COLS], f32)
        prow = sb(pa, "place_partition", [P, NG * 2], f32)
        pcol = sb(pa, "place_column", [P, NG * 2], f32)
        st = sb(pa, "bn_stats", [P, 2, TB, 6], f32)
        mv = sb(pa, "mean_var_steps", [P, 5, TB], f32)
        mu = sb(pa, "mean", [P, 2, TB], f32)
        ve = sb(pa, "var_eps", [P, 2, TB], f32)
        sd = sb(pa, "std", [P, 2, TB], f32)
        nw = sb(pa, "newton", [P, 4, TB], f32)
        rs = sb(pa, "scaled_rstd", [P, 2, TB], f32)
        zz = sb(pa, "attention_den", [P, 2, TB], f32)
        kr = sb(pa, "k_relu", [P, 2, C], f32)
        vs = sb(pa, "v_parts", [P, 2, TB, C], f16)
        p1 = ExitStack()
        xn = sb(p1, "normed", [P, TB, C], f32)
        xhl = sb(p1, "normed_parts", [P, 2, TB, 2, C], f16)
        rr = sb(p1, "router_hidden", [HID, 2, SEQ], f32)
        p1.close()
        p2 = ExitStack()
        qr = sb(p2, "q_relu", [P, 2, SEQ], f32)
        qs = sb(p2, "q_parts", [P, 2, 2, 2, SEQ], f16)
        ks = sb(p2, "k_parts", [P, 2, TB, C], f16)
        pa.push(p2)
        pr = ExitStack()
        L = sb(pr, "logits", [P, NG, E], f32)
        tm = sb(pr, "route_compare", [P, max(NG * E, NT * E)], f32)
        tb = sb(pr, "route_b", [P, NG, E], f32)
        M1 = sb(pr, "first_choice", [P, NG, E], f32)
        M2 = sb(pr, "second_choice", [P, NG, E], f32)
        cx = sb(pr, "chosen", [P, NG + 1, E], f16)
        iota_e = sb(pr, "iota_expert", [P, NG, E], f32)
        sm = sb(pr, "route_small", [P, 12, NG], f32)
        iota_m = sb(pr, "iota_tiles", [P, E, 16], f32)
        cum = sb(pr, "tiles_before", [P, 4, 2 * E], f32)
        iota_j = sb(pr, "iota_tile", [1, NT, E], f32)
        ej = sb(pr, "tile_expert_f32", [1, 2, NT], f32)
        posf = sb(pr, "places_f32", [P, NG, 2], f32)
        pint = sb(pr, "places_int", [P, 3, NG * 2], i32)
        pr.close()
        ta = tm[:, 0:NG * E].rearrange("p (g e) -> p g e", e=E)
        cmp_m = tm[:, 0:E * 16].rearrange("p (e m) -> p e m", m=16)
        cmp_j = tm[0:1, 0:NT * E].rearrange("p (j e) -> p j e", e=E)
        kvT = sb(pa, "kv_parts", [P, 2, 2, C], f16)
        kvo = sb(pa, "kv_out_parts", [P, 2, 2, C + 4], f16)
        oh = sb(pa, "one_hots", [P, TB * 2, P + 2 * COLS], f16)
        pa.close()

        ident3 = sb(ctx, "ident3", [P, P], f16)
        idxc = sb(ctx, "gather_rows", [P, 2, 2], i32)
        idxy = sb(ctx, "gather_places", [P, 2, 4], i32)
        xg = sb(ctx, "gathered", [P, 2, 2, 2 * C], f16)
        xt = sb(ctx, "gathered_T", [P, 2, 4, TILE], f16)
        hb = sb(ctx, "hidden", [P, 2, 2 * TILE], f32)
        hs = sb(ctx, "hidden_parts", [P, 2, 2, 8, TILE], f16)
        b2b = sb(ctx, "b2_rows", [P, E + 1, C], f32)
        yg = sb(ctx, "expert_rows", [P, 2, 4, C], f32)
        bob = yg[:, 0, 0, :]
        ysb = [xs[:, q, 0:2 * C] for q in range(2)]
        bsb = [stage[:, q, 0:2 * C] for q in range(2)]

        bank = [ctx.enter_context(nc.psum_tensor(f"bank{i}", [P, 512], f32)) for i in range(8)]

        def bank16(i):
            return bank[i][:, :].bitcast(f16)

        consts_up, small_in, b2_in = sem("consts_up"), sem("small_in"), sem("b2_in")
        bsum_done, ident3_up = sem("bsum_done"), sem("ident3_up")
        w_in, w_hi, w_lo = sem2("weight_loaded"), sem("weight_hi_done"), sem("weight_lo_done")
        wr_hi, wr_lo = sem("router_weight_hi"), sem("router_weight_lo")
        x_in, rows_st = sem2("x_loaded"), sem2("rows_stored")
        stats_d, aggr_d, var_d, sd_d = sem("bn_stats_done"), sem("bn_aggr_done"), sem("var_done"), sem("std_done")
        nw_d, xn_d, xhi_d, xlo_d = sem("newton_step"), sem("normed_done"), sem("normed_hi_done"), sem("normed_lo_done")
        tr_d, xth_d, xtl_d = sem("transposed"), sem("xT_hi_done"), sem("xT_lo_done")
        hid_d, r_d, lg_d = sem("router_hidden_done"), sem("router_relu_done"), sem("logits_done")
        chain, rexp, rank_d, route_d, cx_d, dif_d = (sem("route_step"), sem("route_exp"), sem("rank_done"),
                                                    sem("route_done"), sem("chosen_done"), sem("route_dif"))
        q_ps, qr_d, q_hi, q_lo = sem("q_product"), sem("q_relu_done"), sem("q_hi_done"), sem("q_lo_done")
        kv_ps, kr_d, kv_hi, kv_lo = sem("kv_product"), sem("k_relu_done"), sem("kv_hi_done"), sem("kv_lo_done")
        kt_ps, kt_hi, kt_lo = sem("kvT_product"), sem("kvT_hi_done"), sem("kvT_lo_done")
        ko_ps, ko_hi, ko_lo = sem("kvo_product"), sem("kvo_hi_done"), sem("kvo_lo_done")
        n_ps, n_d, den_d, z_d = sem("num_product"), sem("attended"), sem("den_done"), sem("z_done")
        x2_in, base_st = sem2("x_again_loaded"), sem2("base_stored")
        oh_d, tab_ps, tab_d, tab_c = sem("one_hots_done"), sem("list_product"), sem("list_added"), sem("list_step")
        list_d = sem("list_done")
        idx_d, xg_in, tr3_d, xt_d = sem("gather_rows_done"), sem2("gathered_in"), sem("gathered_transposed"), sem("gathered_T_done")
        up_ps, h_d, h_hi, h_lo = sem("up_product"), sem("silu_done"), sem("hidden_hi_done"), sem("hidden_lo_done")
        y_ps, y_ev, ys_st = sem("down_product"), sem("down_evacuated"), sem2("y_stored")
        idy_d, yg_in, bs_in = sem("gather_places_done"), sem2("expert_rows_in"), sem2("base_in")
        cb, cb_d, out_st = sem("combine_step"), sem("combined"), sem2("out_stored")

        block = ctx.enter_context(nc.Block())

        def xT(b, part):
            return Wt[:, ds(XT0 + b, 1), part, :].rearrange("p a n -> p (a n)")

        def xT_at(b, part, c, lo, n):
            return Wt[:, ds(XT0 + b, 1), part, c * SEQ + lo:c * SEQ + lo + n].rearrange("p a n -> p (a n)")

        def chunk_of(c, part):
            return Wt[:, ds(c, 1), part, :].rearrange("p a n -> p (a n)")

        @block.sync
        def _(sp):
            for dst, src in ((Wrf[:, :, :], wr), (wr2s[:, :], wr2), (br1s[:, :], br1), (b1s[:, :], b1),
                             (br2s[:, :], br2.to_broadcast([P, E]))):
                sp.dma_start(dst, src).then_inc(small_in, 16)
            for b in range(2):
                sp.dma_start(xs[:, b, :], x_v[b]).then_inc(x_in[b], 16)
            def rows_out(b, q):
                sp.wait_ge(xlo_d, b + 1)
                sp.dma_start(rows_v[ds(b, 1)].rearrange("a p n -> (a p) n"),
                             xhl[:, q, :, :, :].rearrange("p t s c -> p (t s c)")).then_inc(rows_st[q], 16)
            with sp.Fori(0, NB // 2 - 1) as g:
                for q in range(2):
                    b = g * 2 + q
                    rows_out(b, q)
                    sp.wait_ge(xn_d, b + 1)
                    sp.dma_start(xs[:, q, :], x_v[ds(b + 2, 1)].rearrange("a p n -> (a p) n")).then_inc(x_in[q], 16)
            for b in (NB - 2, NB - 1):
                rows_out(b, b % 2)
            sp.wait_ge(xn_d, NB)
            for b in range(2):
                sp.dma_start(xs[:, b, :], x_v[b]).then_inc(x2_in[b], 16)

            def base_out(b, q):
                sp.wait_ge(n_d, b * 4 + 8)
                sp.dma_start(base_v[ds(b, 1)].rearrange("a p n -> (a p) n"), xs[:, q, :]).then_inc(base_st[q], 16)
            with sp.Fori(0, NB // 2 - 1) as g:
                for q in range(2):
                    b = g * 2 + q
                    base_out(b, q)
                    sp.wait_ge(base_st[q], g * 16 + 16)
                    sp.dma_start(xs[:, q, :], x_v[ds(b + 2, 1)].rearrange("a p n -> (a p) n")).then_inc(x2_in[q], 16)
            for b in (NB - 2, NB - 1):
                base_out(b, b % 2)
            sp.wait_ge(list_d, 1)
            sp.dma_start(b2b[:, :, :].rearrange("p e c -> p (e c)"),
                         b2.to_broadcast([P, (E + 1) * C])).then_inc(b2_in, 16)
            sp.dma_start(bob, bo.to_broadcast([P, C])).then_inc(b2_in, 16)

            def y_out(j, q):
                sp.wait_ge(y_ev, j + 3)
                sp.dma_start(ys_v[ds(j, 1)].rearrange("a p n -> (a p) n"), ysb[q]).then_inc(ys_st[q], 16)
            with sp.Fori(0, NT // 2) as g:
                for q in range(2):
                    y_out(g * 2 + q, q)
            y_out(NT - 1, 0)
            sp.wait_ge(w_lo, 2 + (E + 1) * CE)
            for u in range(2):
                sp.wait_ge(base_st[u], NB // 2 * 16)
            for u in range(2):
                sp.dma_start(bsb[u], base_s[u, 0]).then_inc(bs_in[u], 16)

            def out_out(g, u):
                sp.wait_ge(cb_d, g * 2 + u + 3)
                sp.dma_start(out_s[u, ds(g, 1)].rearrange("a p n -> (a p) n"),
                             ysb[(u + 1) % 2]).then_inc(out_st[u], 16)
            with sp.Fori(0, NS // 2 - 1) as g:
                for u in range(2):
                    out_out(g, u)
                    sp.dma_start(bsb[u], base_s[u, ds(g + 1, 1)].rearrange("a p n -> (a p) n")).then_inc(bs_in[u], 16)
            for u in range(2):
                out_out(NS // 2 - 1, u)
            for u in range(2):
                sp.wait_ge(out_st[u], NS // 2 * 16)

        @block.gpsimd
        def _(pool):
            for q in range(2):
                pool.sem_inc(rows_st[q], 16)
                pool.sem_inc(ys_st[q], 16)
            pool.sem_inc(n_d, 4)
            pool.sem_inc(tab_d, 1)
            pool.sem_inc(tr3_d, 2)
            pool.sem_inc(h_lo, 2)
            pool.sem_inc(y_ev, 2)
            pool.sem_inc(cb_d, 2)
            pool.memset(ident[:, :], 0.0)
            pool.memset(before[:, :], 1.0)
            pool.memset(ones[:, :], 1.0)
            pool.memset(cx[:, NG, :], 0.0)
            pool.memset(cum[:, :, :], 0.0)
            pool.memset(half[:, :], 0.5)
            pool.memset(list_f[:, :], 0.0).then_inc(consts_up, 1)
            pool.wait_ge(consts_up, 1)
            pool.affine_select(out=ident[:, :], in_=ident[:, :], compare_op=ALU.not_equal, fill=1.0,
                               base=0, pattern=[[-1, P]], channel_multiplier=1)
            pool.affine_select(out=before[:, :], in_=before[:, :], compare_op=ALU.is_gt, fill=0.0,
                               base=0, pattern=[[1, P]], channel_multiplier=-1)
            pool.iota(iota_e[:, :, :], pattern=[[0, NG], [1, E]], base=0, channel_multiplier=0,
                      allow_small_or_imprecise_dtypes=True)
            pool.iota(iota_m[:, :, :], pattern=[[0, E], [TILE, 16]], base=0, channel_multiplier=0,
                      allow_small_or_imprecise_dtypes=True)
            pool.iota(iota_j[:, :, :], pattern=[[1, NT], [0, E]], base=0, channel_multiplier=0,
                      allow_small_or_imprecise_dtypes=True)
            pool.iota(iota_p[:, :], pattern=[[1, P]], base=0, channel_multiplier=0,
                      allow_small_or_imprecise_dtypes=True)
            pool.iota(iota_c[:, :], pattern=[[1, COLS]], base=0, channel_multiplier=0,
                      allow_small_or_imprecise_dtypes=True)
            pool.iota(tok_l[:, :], pattern=[[1, TB]], base=0, channel_multiplier=TB,
                      allow_small_or_imprecise_dtypes=True)
            pool.iota(tok_b[:, :], pattern=[[SEQ, NB]], base=0, channel_multiplier=0,
                      allow_small_or_imprecise_dtypes=True).then_inc(consts_up, 1)
            for q in range(2):
                pool.dma_start(stage[:, q, :], wa[q]).then_inc(w_in[q], 16)
            with pool.Fori(0, (E + 1) * CE // 2) as g:
                for q in range(2):
                    pool.wait_ge(w_lo, g * 2 + q + 1)
                    pool.dma_start(stage[:, q, :],
                                   wts[ds(g * 2 + q, 1)].rearrange("a p n -> (a p) n")).then_inc(w_in[q], 16)
            pool.wait_ge(list_d, 1)
            pool.memset(ident3[:, :], 0.0).then_inc(ident3_up, 1)
            pool.wait_ge(ident3_up, 1)
            pool.affine_select(out=ident3[:, :], in_=ident3[:, :], compare_op=ALU.not_equal, fill=1.0,
                               base=0, pattern=[[-1, P]], channel_multiplier=1).then_inc(ident3_up, 1)

            def gather(j, q):
                pool.wait_ge(tr3_d, j + 1)
                pool.tensor_copy(idxc[:, q, :], list_i[:, ds(j * 2, 2)]).then_inc(idx_d, 1)
                for r in range(2):
                    pool.wait_ge(rows_st[r], (NB // 2 + 1) * 16)
                pool.wait_ge(idx_d, j + 1)
                for h in range(2):
                    pool.indirect_dma_start(
                        out=xg[:, q, h, :], out_offset=None, in_=rows_d[:, :],
                        in_offset=bass.IndirectOffsetOnAxis(ap=idxc[:, q, h:h + 1], axis=0)).then_inc(xg_in[q], 16)
            with pool.Fori(0, NT // 2) as g:
                for q in range(2):
                    gather(g * 2 + q, q)
            gather(NT - 1, 0)

            def shared_rows(g, u):
                j = g * 2 + (NT + u)
                pool.wait_ge(tr3_d, j + 1)
                q = (NT + u) % 2
                pool.dma_start(xg[:, q, :, :].rearrange("p h n -> p (h n)"),
                               rows_s[u, ds(g, 1)].rearrange("a p n -> (a p) n")).then_inc(xg_in[q], 32)

            def expert_rows(g, u):
                f = g * 2 + u
                pool.wait_ge(cb_d, f + 1)
                pool.tensor_copy(idxy[:, u, :], pos_i[:, ds(f * 4, 4)]).then_inc(idy_d, 1)
                pool.wait_ge(ys_st[0], (NT // 2 + 2) * 16)
                pool.wait_ge(ys_st[1], (NT // 2 + 1) * 16)
                pool.wait_ge(idy_d, f + 1)
                for k in range(4):
                    pool.indirect_dma_start(
                        out=yg[:, u, k, :], out_offset=None, in_=ys_d[:, :],
                        in_offset=bass.IndirectOffsetOnAxis(ap=idxy[:, u, k:k + 1], axis=0)).then_inc(yg_in[u], 16)
            for u in range(2):
                shared_rows(0, u)
            shared_rows(1, 0)
            expert_rows(0, 0)
            shared_rows(1, 1)
            expert_rows(0, 1)
            with pool.Fori(1, NS // 2 - 1) as g:
                for u in range(2):
                    shared_rows(g + 1, u)
                    expert_rows(g, u)
            for u in range(2):
                expert_rows(NS // 2 - 1, u)

        @block.scalar
        def _(act):
            def split_hi(n, q, dst, g):
                act.wait_ge(w_in[q], g * 16 + 16)
                nc.scalar.activation(dst, stage[:, q, :], ACT.Copy, scale=S_W).then_inc(w_hi, 1)

            act.preload_act_table(ACT.Sqrt)
            act.wait_ge(small_in, 80)
            nc.scalar.activation(Wr[:, 0, :, :], Wrf[:, :, :], ACT.Copy, scale=S_W).then_inc(wr_hi, 1)

            def std(b, q):
                act.wait_ge(var_d, b + 1)
                nc.scalar.activation(sd[:, q, :], ve[:, q, :], ACT.Sqrt).then_inc(sd_d, 1)

            def phase1(b, q, g, more):
                act.wait_ge(xn_d, b + 1)
                act.wait_ge(rows_st[q], g * 16 + 16)
                nc.scalar.activation(xhl[:, q, :, 0, :], xn[:, :, :], ACT.Copy).then_inc(xhi_d, 1)
                if more:
                    std(b + 1, 1 - q)
                act.wait_ge(tr_d, b * 2 + 2)
                nc.scalar.activation(xT(b, 0), bank16(2 * q), ACT.Copy).then_inc(xth_d, 1)
                act.wait_ge(hid_d, b + 1)
                nc.scalar.activation(rr[:, q, :], bank[5 + q][0:HID, :], ACT.Relu, bias=br1s[:, 0:1],
                                     scale=1.0 / (S_X * S_W)).then_inc(r_d, 1)
                split_hi(b + 2, q, chunk_of(b, 0), g + 1)

            std(0, 0)
            for q in range(2):
                split_hi(q, q, Wa[:, q, 0, :], 0)
            with act.Fori(0, NB // 2 - 1) as g:
                for q in range(2):
                    phase1(g * 2 + q, q, g, True)
            phase1(NB - 2, 0, NB // 2 - 1, True)
            phase1(NB - 1, 1, NB // 2 - 1, False)

            act.preload_act_table(ACT.Exp)
            act.wait_ge(dif_d, 1)
            nc.scalar.activation(tb[:, :, :], ta, ACT.Exp).then_inc(rexp, 1)
            act.wait_ge(dif_d, 2)
            nc.scalar.activation(sm[:, 5, :], sm[:, 4, :], ACT.Exp).then_inc(rexp, 1)
            act.wait_ge(dif_d, 3)
            nc.scalar.activation(sm[:, 9, :], sm[:, 8, :], ACT.Exp, scale=0.5).then_inc(rexp, 1)

            SC = S_Q / (S_X * S_W)

            def q_parts(b, q, first=False):
                for h in range(2):
                    act.wait_ge(q_ps, b * 2 + h + 1)
                    if not first:
                        act.wait_ge(q_lo, b * 2 + h - 1)
                    nc.scalar.activation(qr[:, h, :], bank[h][:, :], ACT.Relu, scale=SC).then_inc(qr_d, 1)
                    act.wait_ge(qr_d, b * 2 + h + 1)
                    nc.scalar.activation(qs[:, q, 0, h, :], qr[:, h, :], ACT.Copy, bias=EPS * S_Q).then_inc(q_hi, 1)

            def kv_parts(b):
                for t in range(TB):
                    act.wait_ge(kv_ps, b * 4 + t + 1)
                    nc.scalar.activation(kr[:, t % 2, :], bank[2 + t % 2][:, 0:C], ACT.Relu, scale=SC).then_inc(kr_d, 1)
                    nc.scalar.activation(vs[:, 0, t, :], bank[2 + t % 2][:, C:2 * C], ACT.Copy, scale=SC)
                    act.wait_ge(kr_d, b * 4 + t + 1)
                    nc.scalar.activation(ks[:, 0, t, :], kr[:, t % 2, :], ACT.Copy, bias=EPS * S_Q).then_inc(kv_hi, 1)

            def phase2(b, q, g, more):
                def chunk(i):
                    turn = 5 + 3 * q // 2 + (i + q % 2) // 2 if q == 0 else 5 + (3 + i) // 2
                    split_hi(None, (q + i) % 2, chunk_of(b * 3 + (8 + i), 0), g * 3 + turn)
                act.wait_ge(kt_ps, b + 1)
                nc.scalar.activation(kvT[:, 0, :, :], bank[4][:, :].rearrange("p (h d) -> p h d", h=2), ACT.Copy,
                                     scale=S_KV / (S_Q * S_Q)).then_inc(kt_hi, 1)
                if more:
                    q_parts(b + 1, 1 - q)
                chunk(0)
                act.wait_ge(ko_ps, b + 1)
                for h in range(2):
                    ins = nc.scalar.activation(kvo[:, 0, h, 0:C + 1], bank[5 + h][:, 0:C + 1], ACT.Copy, scale=1.0 / S_W)
                ins.then_inc(ko_hi, 1)
                chunk(1)
                if more:
                    kv_parts(b + 1)
                chunk(2)

            act.wait_ge(xlo_d, NB)
            act.wait_ge(lg_d, NB)
            for q in range(2):
                act.wait_ge(rows_st[q], (NB // 2 + 1) * 16)
            q_parts(0, 0, first=True)
            kv_parts(0)
            with act.Fori(0, NB // 2 - 1) as g:
                for q in range(2):
                    phase2(g * 2 + q, q, g, True)
            phase2(NB - 2, 0, NB // 2 - 1, True)
            phase2(NB - 1, 1, NB // 2 - 1, False)

            for i in range(CE):
                n = 2 + E * CE + i
                split_hi(n, n % 2, Wt[:, E * CE + i, 0, :], n // 2)

            act.preload_act_table(ACT.Silu)
            act.wait_ge(list_d, 1)

            def silus(j):
                eb = act.value_load(et[0:1, 2, ds(j, 1)], min_val=0, max_val=8 * E)
                for k in range(4):
                    act.wait_ge(up_ps, j * 4 + k + 1)
                    act.wait_ge(h_lo, j * 4 + k + 1)
                    for i in range(2):
                        ins = nc.scalar.activation(hb[:, k % 2, i * TILE:(i + 1) * TILE],
                                                   bank[k][:, i * TILE:(i + 1) * TILE], ACT.Silu,
                                                   bias=b1s[:, ds(eb + (2 * k + i), 1)], scale=1.0 / (S_X * S_W))
                    ins.then_inc(h_d, 1)
            with act.Fori(0, NALL) as j:
                silus(j)

        @block.vector
        def _(dve):
            steps = [0]

            def link(ins):
                steps[0] += 1
                ins.then_inc(chain, 1)
                dve.wait_ge(chain, steps[0])

            def split_lo(n, q, hi, lo):
                dve.wait_ge(w_hi, n + 1)
                nc.vector.scalar_tensor_tensor(out=lo, in0=stage[:, q, :], scalar=S_W, in1=hi,
                                               op0=ALU.mult, op1=ALU.subtract).then_inc(w_lo, 1)

            dve.wait_ge(wr_hi, 1)
            nc.vector.scalar_tensor_tensor(out=Wr[:, 1, :, :], in0=Wrf[:, :, :], scalar=S_W, in1=Wr[:, 0, :, :],
                                           op0=ALU.mult, op1=ALU.subtract).then_inc(wr_lo, 1)

            def stats(b, q, g):
                dve.wait_ge(x_in[q], g * 16 + 16)
                for t in range(TB):
                    ins = nc.vector.bn_stats(st[:, q, t, :], xs[:, q, t * C:(t + 1) * C])
                ins.then_inc(stats_d, 1)
                dve.wait_ge(stats_d, b + 1)
                m0, v0, m1, v1 = (st[:, q, :, k] for k in (1, 2, 4, 5))
                nc.vector.tensor_tensor(mv[:, 0, :], m0, m1, ALU.add)
                nc.vector.tensor_tensor(mv[:, 1, :], m0, m1, ALU.subtract)
                nc.vector.tensor_tensor(mv[:, 2, :], v0, v1, ALU.add).then_inc(aggr_d, 1)
                dve.wait_ge(aggr_d, b * 2 + 1)
                nc.vector.tensor_scalar(mu[:, q, :], mv[:, 0, :], 0.5, None, ALU.mult)
                nc.vector.tensor_tensor(mv[:, 3, :], mv[:, 1, :], mv[:, 1, :], ALU.mult)
                nc.vector.tensor_scalar(mv[:, 4, :], mv[:, 2, :], 1.0 / C, LN_EPS, ALU.mult, ALU.add).then_inc(aggr_d, 1)
                dve.wait_ge(aggr_d, b * 2 + 2)
                nc.vector.scalar_tensor_tensor(out=ve[:, q, :], in0=mv[:, 3, :], scalar=0.25, in1=mv[:, 4, :],
                                               op0=ALU.mult, op1=ALU.add).then_inc(var_d, 1)

            def norm(b, q):
                def step(ins, k):
                    ins.then_inc(nw_d, 1)
                    dve.wait_ge(nw_d, b * 5 + k)
                dve.wait_ge(sd_d, b + 1)
                step(nc.vector.reciprocal(nw[:, 0, :], sd[:, q, :]), 1)
                step(nc.vector.tensor_tensor(nw[:, 1, :], nw[:, 0, :], nw[:, 0, :], ALU.mult), 2)
                step(nc.vector.tensor_tensor(nw[:, 2, :], nw[:, 1, :], ve[:, q, :], ALU.mult), 3)
                step(nc.vector.tensor_scalar(nw[:, 3, :], nw[:, 2, :], -0.5 * S_X, 1.5 * S_X, ALU.mult, ALU.add), 4)
                step(nc.vector.tensor_tensor(rs[:, q, :], nw[:, 0, :], nw[:, 3, :], ALU.mult), 5)
                for t in range(TB):
                    ins = nc.vector.tensor_scalar(xn[:, t, :], xs[:, q, t * C:(t + 1) * C], mu[:, q, t:t + 1],
                                                  rs[:, q, t:t + 1], ALU.subtract, ALU.mult)
                ins.then_inc(xn_d, 1)

            def phase1(b, q, g, more):
                if more:
                    stats(b + 1, 1 - q, g + q)
                dve.wait_ge(xhi_d, b + 1)
                nc.vector.tensor_tensor(xhl[:, q, :, 1, :], xn[:, :, :], xhl[:, q, :, 0, :], ALU.subtract).then_inc(xlo_d, 1)
                if more:
                    dve.wait_ge(xlo_d, b + 1)
                    norm(b + 1, 1 - q)
                dve.wait_ge(tr_d, b * 2 + 2)
                nc.vector.tensor_copy(xT(b, 1), bank16(2 * q + 1)).then_inc(xtl_d, 1)
                split_lo(b + 2, q, chunk_of(b, 0), chunk_of(b, 1))

            stats(0, 0, 0)
            norm(0, 0)
            for q in range(2):
                split_lo(q, q, Wa[:, q, 0, :], Wa[:, q, 1, :])
            with dve.Fori(0, NB // 2 - 1) as g:
                for q in range(2):
                    phase1(g * 2 + q, q, g, True)
            phase1(NB - 2, 0, NB // 2 - 1, True)
            phase1(NB - 1, 1, NB // 2 - 1, False)

            V = nc.vector

            def over_e(small):
                return small.rearrange("p (g a) -> p g a", a=1).to_broadcast([P, NG, E])
            m1, a1, m2, a2, d2, x2, z, g2, dd, uu, den, tmp = (sm[:, k, :] for k in range(12))
            dve.wait_ge(lg_d, NB)
            dve.wait_ge(consts_up, 2)
            link(V.tensor_tensor(L[:, :, :], bank[4][:, 0:NG * E].rearrange("p (g e) -> p g e", e=E),
                                 br2s[:, :].rearrange("p (a e) -> p a e", a=1).to_broadcast([P, NG, E]), ALU.add))

            def choose(best, mask, at):
                link(V.tensor_reduce(best, L[:, :, :], AX.X, ALU.max))
                link(V.tensor_tensor(ta, L[:, :, :], over_e(best), ALU.is_equal))
                link(V.scalar_tensor_tensor(out=ta, in0=ta, scalar=-float(E), in1=iota_e[:, :, :],
                                            op0=ALU.mult, op1=ALU.add))
                link(V.tensor_reduce(at, ta, AX.X, ALU.min))
                link(V.tensor_tensor(mask, ta, over_e(at), ALU.is_equal))
            choose(m1, M1[:, :, :], a1)
            V.tensor_tensor(ta, L[:, :, :], over_e(m1), ALU.subtract).then_inc(dif_d, 1)
            dve.wait_ge(rexp, 1)
            link(V.tensor_reduce(tmp, tb[:, :, :], AX.X, ALU.add))
            link(V.reciprocal(z, tmp))
            link(V.scalar_tensor_tensor(out=L[:, :, :], in0=M1[:, :, :], scalar=-1e30, in1=L[:, :, :],
                                        op0=ALU.mult, op1=ALU.add))
            choose(m2, M2[:, :, :], a2)
            V.tensor_tensor(d2, m2, m1, ALU.subtract).then_inc(dif_d, 1)
            V.tensor_tensor(cx[:, 0:NG, :], M1[:, :, :], M2[:, :, :], ALU.add).then_inc(cx_d, 1)
            dve.wait_ge(rexp, 2)
            link(V.tensor_tensor(g2, x2, z, ALU.mult))
            V.tensor_tensor(dd, g2, z, ALU.subtract).then_inc(dif_d, 1)
            dve.wait_ge(rexp, 3)
            link(V.tensor_scalar_add(den, uu, 1.0))
            link(V.reciprocal(wc[:, :, 0], den))
            link(V.tensor_tensor(wc[:, :, 1], uu, wc[:, :, 0], ALU.mult))
            dve.wait_ge(rank_d, 1)
            rank = bank[7][:, 0:(NG + 1) * E].rearrange("p (g e) -> p g e", e=E)
            link(V.tensor_copy(cum[:, 3, 0:E], rank[:, NG, :]))
            link(V.tensor_tensor(cmp_m, cum[:, 3, 0:E].rearrange("p (e a) -> p e a", a=1).to_broadcast([P, E, 16]),
                                 iota_m[:, :, :], ALU.is_gt))
            link(V.tensor_reduce(cum[:, 0, E:2 * E], cmp_m, AX.X, ALU.add))
            for k, (s, d) in zip((1, 2, 4), ((0, 1), (1, 2), (2, 0))):
                link(V.tensor_tensor(cum[:, d, E:2 * E], cum[:, s, E:2 * E], cum[:, s, E - k:2 * E - k], ALU.add))
            link(V.tensor_tensor(cmp_j, iota_j[:, :, :],
                                 cum[0:1, 0, E:2 * E].rearrange("p (a e) -> p a e", a=1).to_broadcast([1, NT, E]), ALU.is_ge))
            link(V.tensor_reduce(ej[:, 0, :], cmp_j, AX.X, ALU.add))
            link(V.tensor_scalar_min(ej[:, 1, :], ej[:, 0, :], float(E - 1)))
            link(V.memset(et[:, :, NT:NALL + 1], 0))
            for k, by in enumerate((1, CE, 8)):
                link(V.tensor_scalar(et[:, k, 0:NT], ej[:, 1, :], float(by), None, ALU.mult))
                link(V.tensor_scalar_add(et[:, k, NT:NALL], et[:, k, NT:NALL], float(by * E)))
            link(V.scalar_tensor_tensor(out=tb[:, :, :], scalar=float(TILE), in1=rank[:, 0:NG, :],
                                        in0=cum[:, 0, E - 1:2 * E - 1].rearrange("p (a e) -> p a e", a=1).to_broadcast([P, NG, E]),
                                        op0=ALU.mult, op1=ALU.add))
            for s, mask in enumerate((M1, M2)):
                link(V.tensor_tensor(ta, mask[:, :, :], tb[:, :, :], ALU.mult))
                link(V.tensor_reduce(posf[:, :, s], ta, AX.X, ALU.add))
            link(V.tensor_copy(pos_i[:, :], posf[:, :, :].rearrange("p g s -> p (g s)")))
            link(V.tensor_scalar(pint[:, 0, :], pos_i[:, :], 1, P - 1, ALU.logical_shift_right, ALU.bitwise_and))
            link(V.tensor_scalar(pint[:, 1, :], pos_i[:, :], 8, 1, ALU.logical_shift_right, ALU.logical_shift_left))
            link(V.tensor_scalar(pint[:, 2, :], pos_i[:, :], 1, None, ALU.bitwise_and))
            link(V.tensor_copy(prow[:, :], pint[:, 0, :]))
            link(V.tensor_tensor(pcol[:, :], pint[:, 1, :], pint[:, 2, :], ALU.add))

            SC = S_Q / (S_X * S_W)

            def q_parts(b, q):
                for h in range(2):
                    dve.wait_ge(q_hi, b * 2 + h + 1)
                    V.scalar_tensor_tensor(out=qs[:, q, 1, h, :], in0=qr[:, h, :], scalar=EPS * S_Q, in1=qs[:, q, 0, h, :],
                                           op0=ALU.add, op1=ALU.subtract).then_inc(q_lo, 1)

            def kv_parts(b):
                for t in range(TB):
                    dve.wait_ge(kv_hi, b * 4 + t + 1)
                    V.scalar_tensor_tensor(out=vs[:, 1, t, :], in0=bank[2 + t % 2][:, C:2 * C], scalar=SC, in1=vs[:, 0, t, :],
                                           op0=ALU.mult, op1=ALU.subtract)
                    V.scalar_tensor_tensor(out=ks[:, 1, t, :], in0=kr[:, t % 2, :], scalar=EPS * S_Q, in1=ks[:, 0, t, :],
                                           op0=ALU.add, op1=ALU.subtract).then_inc(kv_lo, 1)

            def one_hots(b):
                dve.wait_ge(tab_d, b + 1)
                for t in range(TB):
                    for s in range(2):
                        k = t * 2 + s
                        V.tensor_scalar(oh[:, k, 0:P], iota_p[:, :], prow[:, ds(b * 8 + k, 1)], None, ALU.is_equal)
                        V.tensor_scalar(oh[:, k, P:P + COLS], iota_c[:, :], pcol[:, ds(b * 8 + k, 1)], tok_l[:, t:t + 1],
                                        ALU.is_equal, ALU.mult)
                        ins = V.tensor_scalar(oh[:, k, P + COLS:], iota_c[:, :], pcol[:, ds(b * 8 + k, 1)], None, ALU.is_equal)
                ins.then_inc(oh_d, 1)

            def add_list(b):
                dve.wait_ge(tab_ps, b + 1)
                V.scalar_tensor_tensor(out=list_f[:, :], in0=bank[7][:, COLS:2 * COLS], scalar=tok_b[:, ds(b, 1)],
                                       in1=list_f[:, :], op0=ALU.mult, op1=ALU.add).then_inc(tab_c, 1)
                dve.wait_ge(tab_c, b + 1)
                V.tensor_tensor(list_f[:, :], bank[7][:, 0:COLS], list_f[:, :], ALU.add).then_inc(tab_d, 1)

            def attend(b, q, g):
                dve.wait_ge(x2_in[q], g * 16 + 16)
                for t in range(TB):
                    num = bank[7 if t % 2 == 0 else 4]
                    dve.wait_ge(n_ps, b * 4 + t + 1)
                    V.tensor_scalar_add(zz[:, 0, t:t + 1], num[:, C:C + 1], EPS * S_Q * S_KV).then_inc(den_d, 1)
                    dve.wait_ge(den_d, b * 4 + t + 1)
                    V.reciprocal(zz[:, 1, t:t + 1], zz[:, 0, t:t + 1]).then_inc(z_d, 1)
                    dve.wait_ge(z_d, b * 4 + t + 1)
                    V.scalar_tensor_tensor(out=xs[:, q, t * C:(t + 1) * C], in0=num[:, 0:C], scalar=zz[:, 1, t:t + 1],
                                           in1=xs[:, q, t * C:(t + 1) * C], op0=ALU.mult, op1=ALU.add).then_inc(n_d, 1)

            def phase2(b, q, g, more):
                def chunk(i):
                    c = b * 3 + (8 + i)
                    split_lo(c + 2, (q + i) % 2, chunk_of(c, 0), chunk_of(c, 1))
                dve.wait_ge(kt_hi, b + 1)
                V.scalar_tensor_tensor(out=kvT[:, 1, :, :], in0=bank[4][:, :].rearrange("p (h d) -> p h d", h=2),
                                       scalar=S_KV / (S_Q * S_Q), in1=kvT[:, 0, :, :],
                                       op0=ALU.mult, op1=ALU.subtract).then_inc(kt_lo, 1)
                if more:
                    q_parts(b + 1, 1 - q)
                chunk(0)
                dve.wait_ge(ko_hi, b + 1)
                for h in range(2):
                    ins = V.scalar_tensor_tensor(out=kvo[:, 1, h, 0:C + 1], in0=bank[5 + h][:, 0:C + 1], scalar=1.0 / S_W,
                                                 in1=kvo[:, 0, h, 0:C + 1], op0=ALU.mult, op1=ALU.subtract)
                ins.then_inc(ko_lo, 1)
                one_hots(b)
                chunk(1)
                if more:
                    kv_parts(b + 1)
                attend(b, q, g)
                chunk(2)
                add_list(b)

            q_parts(0, 0)
            kv_parts(0)
            with dve.Fori(0, NB // 2 - 1) as g:
                for q in range(2):
                    phase2(g * 2 + q, q, g, True)
            phase2(NB - 2, 0, NB // 2 - 1, True)
            phase2(NB - 1, 1, NB // 2 - 1, False)
            dve.wait_ge(tab_d, NB + 1)
            V.tensor_copy(list_i[:, :], list_f[:, :]).then_inc(list_d, 1)
            for i in range(CE):
                n = 2 + E * CE + i
                split_lo(n, n % 2, Wt[:, E * CE + i, 0, :], Wt[:, E * CE + i, 1, :])

            dve.wait_ge(list_d, 1)

            def rows_T(j, q):
                dve.wait_ge(tr3_d, j + 3)
                V.tensor_copy(xt[:, q, :, :].rearrange("p s n -> p (s n)"), bank16(4 + q)).then_inc(xt_d, 1)

            def h_parts(j, q):
                for k in range(4):
                    dve.wait_ge(h_d, j * 4 + k + 1)
                    hk = hb[:, k % 2, :].rearrange("p (i n) -> p i n", i=2)
                    V.tensor_scalar(hs[:, q, 0, 2 * k:2 * k + 2, :], hk, S_H, None, ALU.mult).then_inc(h_hi, 1)
                    dve.wait_ge(h_hi, j * 4 + k + 1)
                    V.scalar_tensor_tensor(out=hs[:, q, 1, 2 * k:2 * k + 2, :].rearrange("p i n -> p (i n)"), in0=hb[:, k % 2, :],
                                           scalar=S_H, in1=hs[:, q, 0, 2 * k:2 * k + 2, :].rearrange("p i n -> p (i n)"),
                                           op0=ALU.mult, op1=ALU.subtract).then_inc(h_lo, 1)

            def y_plus_b2(q, b2_row):
                V.scalar_tensor_tensor(out=ysb[q].rearrange("p (h c) -> p h c", h=2),
                                       in0=bank[6 + q][:, :].rearrange("p (h c) -> p h c", h=2),
                                       scalar=1.0 / (S_H * S_W), in1=b2_row.to_broadcast([P, 2, C]),
                                       op0=ALU.mult, op1=ALU.add).then_inc(y_ev, 1)

            def y_rows(j, q, g):
                ev = dve.value_load(et[0:1, 0, ds(j, 1)], min_val=0, max_val=E)
                dve.wait_ge(y_ps, j + 1)
                dve.wait_ge(ys_st[q], g * 16 + 16)
                y_plus_b2(q, b2b[:, ds(ev, 1), :])

            def expert_tile(j, q, g):
                h_parts(j + 1, 1 - q)
                rows_T(j + 2, q)
                y_rows(j, q, g)

            rows_T(0, 0)
            rows_T(1, 1)
            h_parts(0, 0)
            dve.wait_ge(b2_in, 32)
            dve.wait_ge(base_st[0], NB // 2 * 16)
            dve.wait_ge(base_st[1], NB // 2 * 16)
            V.tensor_tensor(b2b[:, E, :], b2b[:, E, :], bob, ALU.add).then_inc(bsum_done, 1)
            with dve.Fori(0, NT // 2) as g:
                for q in range(2):
                    expert_tile(g * 2 + q, q, g)
            expert_tile(NT - 1, 0, NT // 2)
            dve.wait_ge(bsum_done, 1)

            def shared_tile(g, u, ahead):
                q = (NT + u) % 2
                f = g * 2 + u
                j = g * 2 + (NT + u)
                if ahead >= 1:
                    h_parts(j + 1, 1 - q)
                if ahead >= 2:
                    rows_T(j + 2, q)

                def step(ins, k):
                    ins.then_inc(cb, 1)
                    dve.wait_ge(cb, f * 2 + k)
                dve.wait_ge(y_ps, j + 1)
                y_plus_b2(q, b2b[:, E:E + 1, :])
                dve.wait_ge(y_ev, j + 3)
                dve.wait_ge(bs_in[u], g * 16 + 16)
                step(V.tensor_tensor(ysb[q], ysb[q], bsb[u], ALU.add), 1)
                dve.wait_ge(yg_in[u], g * 64 + 64)
                for s in range(2):
                    for h in range(2):
                        ins = V.scalar_tensor_tensor(out=ysb[q][:, h * C:(h + 1) * C], in0=yg[:, u, 2 * h + s, :],
                                                     scalar=wc[:, :, :].rearrange("p g s -> p (g s)")[:, ds(f * 4 + (2 * h + s), 1)],
                                                     in1=ysb[q][:, h * C:(h + 1) * C], op0=ALU.mult, op1=ALU.add)
                    if s == 0:
                        step(ins, 2)
                ins.then_inc(cb_d, 1)

            dve.wait_ge(ys_st[1], (NT // 2 + 1) * 16)
            dve.wait_ge(ys_st[0], (NT // 2 + 2) * 16)
            shared_tile(0, 0, 2)
            shared_tile(0, 1, 2)
            with dve.Fori(1, NS // 2 - 1) as g:
                for u in range(2):
                    dve.wait_ge(out_st[u], g * 16)
                    shared_tile(g, u, 2)
            for u in range(2):
                dve.wait_ge(out_st[u], (NS // 2 - 1) * 16)
                shared_tile(NS // 2 - 1, u, 1 - u)

        @block.tensor
        def _(pe):
            mm = nc.tensor.matmul

            def phase1(b, q):
                pe.wait_ge(xlo_d, b + 1)
                for s in range(2):
                    for c in range(2):
                        for t in range(TB):
                            ins = nc.tensor.transpose(bank16(2 * q + s)[:, c * SEQ + t * P:c * SEQ + (t + 1) * P],
                                                      xhl[:, q, t, s, c * P:(c + 1) * P], ident[:, :])
                    ins.then_inc(tr_d, 1)
                pe.wait_ge(xth_d, b + 1)
                pe.wait_ge(xtl_d, b + 1)
                hid = bank[5 + q][0:HID, :]
                for n, (c, sw, sx) in enumerate((c, sw, sx) for c in range(2) for sw, sx in ((0, 0), (0, 1), (1, 0))):
                    ins = mm(hid, Wr[:, sw, c, :], xT_at(b, sx, c, 0, SEQ), start=(n == 0), stop=(n == 5))
                ins.then_inc(hid_d, 1)
                pe.wait_ge(r_d, b + 1)
                for t in range(TB):
                    ins = mm(bank[4][:, ds(b * (TB * E) + t * E, E)], rr[:, q, t * P:(t + 1) * P], wr2s[:, :],
                             start=True, stop=True)
                ins.then_inc(lg_d, 1)

            pe.wait_ge(consts_up, 2)
            pe.wait_ge(wr_lo, 1)
            with pe.Fori(0, NB // 2) as g:
                for q in range(2):
                    phase1(g * 2 + q, q)

            THREE = ((0, 0), (0, 1), (1, 0))

            def q_product(b, first=False):
                for h in range(2):
                    if not first:
                        pe.wait_ge(q_hi, b * 2 + h - 1)
                    for n, (c, a, m) in enumerate((c, a, m) for c in range(2) for a, m in THREE):
                        ins = mm(bank[h][:, :], Wa[:, c, a, h * P:(h + 1) * P], xT_at(b, m, c, 0, SEQ),
                                 start=(n == 0), stop=(n == 5))
                    ins.then_inc(q_ps, 1)

            def kv_product(b, first=False):
                for t in range(TB):
                    if not (first and t < 2):
                        pe.wait_ge(kv_lo, b * 4 + t - 1)
                    for n, (c, a, m) in enumerate((c, a, m) for c in range(2) for a, m in THREE):
                        ins = mm(bank[2 + t % 2][:, :], xT_at(b, a, c, t * P, P), Wa[:, c, m, C:3 * C],
                                 start=(n == 0), stop=(n == 5))
                    ins.then_inc(kv_ps, 1)

            def phase2(b, q, more):
                pe.wait_ge(kv_lo, b * 4 + 4)
                pe.wait_ge(n_d, b * 4 + 4)
                for h in range(2):
                    for n, (t, a, m) in enumerate((t, a, m) for t in range(TB) for a, m in THREE):
                        ins = mm(bank[4][:, h * C:(h + 1) * C], vs[:, a, t, h * P:(h + 1) * P], ks[:, m, t, :],
                                 start=(n == 0), stop=(n == 3 * TB - 1))
                ins.then_inc(kt_ps, 1)
                for h in range(2):
                    for n, (t, a) in enumerate((t, a) for t in range(TB) for a in range(2)):
                        mm(bank[5 + h][:, C:C + 1], ks[:, a, t, h * P:(h + 1) * P], half[:, :],
                           start=(n == 0), stop=(n == 2 * TB - 1))
                if more:
                    q_product(b + 1)
                pe.wait_ge(kt_lo, b + 1)
                for h in range(2):
                    for n, (c, a, m) in enumerate((c, a, m) for c in range(2) for a, m in THREE):
                        ins = mm(bank[5 + h][:, 0:C], kvT[:, a, c, h * P:(h + 1) * P], Wa[:, c, m, 3 * C:4 * C],
                                 start=(n == 0), stop=(n == 5))
                ins.then_inc(ko_ps, 1)
                if more:
                    kv_product(b + 1)
                pe.wait_ge(ko_lo, b + 1)
                pe.wait_ge(q_lo, b * 2 + 2)
                pe.wait_ge(tab_d, b + 1)
                for t in range(TB):
                    if t >= 2:
                        pe.wait_ge(n_d, b * 4 + t + 3)
                    for n, (c, a, m) in enumerate((c, a, m) for c in range(2) for a, m in THREE):
                        ins = mm(bank[7 if t % 2 == 0 else 4][:, 0:C + 1], qs[:, q, a, c, t * P:(t + 1) * P],
                                 kvo[:, m, c, 0:C + 1], start=(n == 0), stop=(n == 5))
                    ins.then_inc(n_ps, 1)
                pe.wait_ge(n_d, b * 4 + 7)
                pe.wait_ge(oh_d, b + 1)
                for k in range(2 * TB):
                    ins = mm(bank[7][:, 0:2 * COLS], oh[:, k, 0:P], oh[:, k, P:], start=(k == 0), stop=(k == 2 * TB - 1))
                ins.then_inc(tab_ps, 1)

            pe.wait_ge(w_lo, 2)
            q_product(0, first=True)
            pe.wait_ge(cx_d, 1)
            flat = cx[:, :, :].rearrange("p g e -> p (g e)")
            mm(bank[7][:, 0:(NG + 1) * E], before[:, :], flat, start=True, stop=False)
            for t in range(NG):
                n = NG - t
                ins = mm(bank[7][:, (t + 1) * E:(NG + 1) * E].rearrange("p (n e) -> p n e", e=E), ones[:, :],
                         cx[:, t:t + 1, :].to_broadcast([P, n, E]), start=False, stop=(t == NG - 1))
            ins.then_inc(rank_d, 1)
            kv_product(0, first=True)
            with pe.Fori(0, NB // 2 - 1) as g:
                for q in range(2):
                    phase2(g * 2 + q, q, True)
            phase2(NB - 2, 0, True)
            phase2(NB - 1, 1, False)

            def rows_T(j, q, g):
                pe.wait_ge(xg_in[q], g * 32 + 32)
                for s in range(4):
                    for h in range(2):
                        ins = nc.tensor.transpose(bank16(4 + q)[:, s * TILE + h * P:s * TILE + (h + 1) * P],
                                                  xg[:, q, h, s * P:(s + 1) * P], ident3[:, :])
                ins.then_inc(tr3_d, 1)

            def up(j, q, first=False):
                e4 = pe.value_load(et[0:1, 1, ds(j, 1)], min_val=0, max_val=CE * E)
                pe.wait_ge(xt_d, j + 1)
                for k in range(4):
                    if not first:
                        pe.wait_ge(h_d, j * 4 + (k - 3))
                    for i in range(2):
                        col = (2 * k + i) * P
                        for n, (c, a, m) in enumerate((c, a, m) for c in range(2) for a, m in THREE):
                            ins = mm(bank[k][:, i * TILE:(i + 1) * TILE],
                                     Wt[:, ds(e4 + c, 1), a, col:col + P].rearrange("p a n -> p (a n)"),
                                     xt[:, q, 2 * m + c, :], start=(n == 0), stop=(n == 5))
                    ins.then_inc(up_ps, 1)

            def down(j, q):
                e4 = pe.value_load(et[0:1, 1, ds(j, 1)], min_val=0, max_val=CE * E)
                pe.wait_ge(h_lo, j * 4 + 6)
                pe.wait_ge(y_ev, j + 1)
                for h in range(2):
                    for n, (i, a, m) in enumerate((i, a, m) for i in range(8) for a, m in THREE):
                        ins = mm(bank[6 + q][:, h * C:(h + 1) * C], hs[:, q, a, i, h * P:(h + 1) * P],
                                 Wt[:, ds(e4 + (2 + i // 4), 1), m, i % 4 * C:(i % 4 + 1) * C].rearrange("p a n -> p (a n)"),
                                 start=(n == 0), stop=(n == 23))
                ins.then_inc(y_ps, 1)

            pe.wait_ge(list_d, 1)
            pe.wait_ge(ident3_up, 2)
            rows_T(0, 0, 0)
            rows_T(1, 1, 0)
            up(0, 0, first=True)
            with pe.Fori(0, (NALL - 3) // 2) as g:
                for q in range(2):
                    j = g * 2 + q
                    up(j + 1, 1 - q)
                    rows_T(j + 2, q, g + 1)
                    down(j, q)
            j = NALL - 3
            up(j + 1, (j + 1) % 2)
            rows_T(j + 2, j % 2, (j + 2) // 2)
            down(j, j % 2)
            up(j + 2, j % 2)
            down(j + 1, (j + 1) % 2)
            down(j + 2, j % 2)


def kernel(L0_attn_x, L0_attn_W_qkv, L0_attn_W_out, L0_attn_b_out, L0_ffn_Wr1, L0_ffn_br1, L0_ffn_Wr2, L0_ffn_br2,
           L0_ffn_Ws1, L0_ffn_bs1, L0_ffn_Ws2, L0_ffn_bs2, L0_ffn_We1, L0_ffn_be1, L0_ffn_We2, L0_ffn_be2):
    import numpy as np
    import concourse.bacc as bacc
    from concourse.bass_utils import run_bass_kernel_spmd

    a = {k: np.asarray(v) for k, v in dict(locals()).items() if k.startswith("L0_")}
    w1 = np.concatenate([a["L0_ffn_We1"], a["L0_ffn_Ws1"][None]])
    w2 = np.concatenate([a["L0_ffn_We2"], a["L0_ffn_Ws2"][None]])
    w1 = w1.reshape(E + 1, 2, P, I)
    w2 = w2.reshape(E + 1, 2, 4, P, C).transpose(0, 1, 3, 2, 4).reshape(E + 1, 2, P, CHUNK)
    b1 = np.concatenate([a["L0_ffn_be1"], a["L0_ffn_bs1"][None]])
    arrays = {
        "x": a["L0_attn_x"].reshape(ROWS, C),
        "wts": np.concatenate([w1, w2], 1).reshape((E + 1) * CE, P, CHUNK),
        "wa": np.concatenate([a["L0_attn_W_qkv"].T, a["L0_attn_W_out"].T], 1).reshape(2, P, CHUNK),
        "wr": a["L0_ffn_Wr1"].reshape(2, P, HID).transpose(1, 0, 2),
        "br1": a["L0_ffn_br1"].reshape(HID, 1),
        "wr2": a["L0_ffn_Wr2"],
        "br2": a["L0_ffn_br2"].reshape(1, E),
        "b1": b1.reshape((E + 1) * 8, P).T,
        "b2": np.concatenate([a["L0_ffn_be2"], a["L0_ffn_bs2"][None]]).reshape(1, (E + 1) * C),
        "bo": a["L0_attn_b_out"].reshape(1, C),
    }
    arrays = {f"in_{k}": np.ascontiguousarray(v) for k, v in arrays.items()}
    nc = bacc.Bacc("TRN2", target_bir_lowering=False, num_devices=1)
    args = [nc.dram_tensor(k, v.shape, mybir.dt.from_np(v.dtype), kind="ExternalInput").ap() for k, v in arrays.items()]
    out = nc.dram_tensor("out_dram", (ROWS, C), mybir.dt.float32, kind="ExternalOutput").ap()
    build_program(nc, *args, out)
    r = run_bass_kernel_spmd(nc, [arrays], core_ids=[0])
    return r.results[0]["out_dram"].reshape(a["L0_attn_x"].shape)
```

```python
import concourse.bass as bass
from concourse import mybir
from contextlib import ExitStack

P = 128
ROWS, C, I, E = 4096, 256, 1024, 8
NB, SEQ = 8, 512
TB = SEQ // P
NG = ROWS // P
HID = C // 4
TILE = 256
NT = (2 * ROWS + E * (TILE - 1)) // TILE
NS = ROWS // TILE
N1 = NS // 2
N2 = N1 + NT
NALL = NT + NS
COLS = NT * 2
CHUNK = 1024
CE = 4
NCH = (E + 1) * CE
CH_OPEN = NCH - 2 * N1
SCR = 24
S_X, S_W, S_Q, S_KV, S_H = 256.0, 256.0, 64.0, 0.125, 64.0
LN_EPS, EPS = 1e-5, 1e-6
THREE = ((0, 0), (0, 1), (1, 0))


def build_program(nc, x, wts, wa, wr, br1, wr2, br2, b1, b2, bo, out):
    f32, f16, i32 = mybir.dt.float32, mybir.dt.float16, mybir.dt.int32
    ALU, ACT, AX = mybir.AluOpType, mybir.ActivationFunctionType, mybir.AxisListType
    ds = bass.ds
    SC = S_Q / (S_X * S_W)

    rows_d = nc.dram_tensor("rows_scratch", (ROWS, 2 * C), f16).ap()
    base_d = nc.dram_tensor("base_scratch", (ROWS, C), f32).ap()
    ys_d = nc.dram_tensor("expert_out_scratch", (NT * TILE, C), f32).ap()
    x_v = x.rearrange("(b p t) c -> b p (t c)", b=NB, t=TB)
    base_v = base_d.rearrange("(b p t) c -> b p (t c)", b=NB, t=TB)
    rows_v = rows_d.rearrange("(b p t) c -> b p (t c)", b=NB, t=TB)
    rows_s = rows_d.rearrange("(b p u h) c -> u b p (h c)", b=NB, u=2, h=2)
    base_s = base_d.rearrange("(b p u h) c -> u b p (h c)", b=NB, u=2, h=2)
    out_s = out.rearrange("(b p u h) c -> u b p (h c)", b=NB, u=2, h=2)
    ys_v = ys_d.rearrange("(j p h) c -> j p (h c)", p=P, h=2)

    ctx = ExitStack()
    with ctx:
        def sem(name):
            return ctx.enter_context(nc.semaphore(name))

        def sem2(name):
            return [sem(name + "_even"), sem(name + "_odd")]

        def sb(stack, name, shape, dt):
            return stack.enter_context(nc.sbuf_tensor(name, shape, dt))

        Wt = sb(ctx, "expert_weights", [P, NCH, 2, CHUNK], f16)
        stage = sb(ctx, "weight_stage", [P, 2, CHUNK], f32)
        xg = sb(ctx, "tile_rows", [P, 2, 2, 2 * C], f16)
        xt = sb(ctx, "tile_rows_T", [P, 2, 4, TILE], f16)
        list_i = sb(ctx, "list_rows", [P, COLS], i32)
        pos_i = sb(ctx, "places", [P, NG * 2], i32)
        wc = sb(ctx, "gate_weights", [P, NG, 2], f32)
        et = sb(ctx, "tile_experts", [1, 3, NT + 1], i32)
        b1s = sb(ctx, "b1_columns", [P, (E + 1) * 8], f32)
        ident = sb(ctx, "ident", [P, P], f16)
        idxc = sb(ctx, "gather_rows", [P, 2, 2], i32)
        idxy = sb(ctx, "gather_places", [P, 2, 2, 4], i32)

        pa = ExitStack()
        xT = sb(pa, "normed_T", [P, 2, 2, 2, SEQ], f16)
        xn = sb(pa, "normed", [P, TB, C], f32)
        xhl = sb(pa, "normed_parts", [P, 2, TB, 2, C], f16)
        rr = sb(pa, "router_hidden", [HID, SEQ], f32)
        qr = sb(pa, "q_relu", [P, 2, SEQ], f32)
        qs = sb(pa, "q_parts", [P, 2, 2, SEQ], f16)
        kr = sb(pa, "k_relu", [P, 2, C], f32)
        ks = sb(pa, "k_parts", [P, 2, TB, C], f16)
        vs = sb(pa, "v_parts", [P, 2, TB, C], f16)
        kvT = sb(pa, "kv_parts", [P, 2, 2, C], f16)
        kvo = sb(pa, "kv_out_parts", [P, 2, 2, C + 4], f16)
        Wrf = sb(pa, "router_w1_f32", [P, 2, HID], f32)
        Wr = sb(pa, "router_w1", [P, 2, 2, HID], f16)
        wr2s = sb(pa, "router_w2", [HID, E], f32)
        br1s = sb(pa, "router_b1", [HID, 1], f32)
        half = sb(pa, "half", [P, 1], f16)
        st = sb(pa, "bn_stats", [P, 2, TB, 6], f32)
        mv = sb(pa, "mean_var_steps", [P, 5, TB], f32)
        mu = sb(pa, "mean", [P, 2, TB], f32)
        ve = sb(pa, "var_eps", [P, 2, TB], f32)
        sd = sb(pa, "std", [P, 2, TB], f32)
        nw = sb(pa, "newton", [P, 4, TB], f32)
        rs = sb(pa, "scaled_rstd", [P, 2, TB], f32)
        zz = sb(pa, "attention_den", [P, 2, TB], f32)
        pa.close()

        hb = sb(ctx, "hidden", [P, 4, 2 * TILE], f32)
        hs = sb(ctx, "hidden_parts", [P, 2, 2, 8, TILE], f16)
        b2b = sb(ctx, "b2_rows", [P, E + 1, C], f32)
        yg = sb(ctx, "expert_rows", [P, 2, 4, C], f32)
        ysb = sb(ctx, "y_rows", [P, 2, 2 * C], f32)
        def gathered(u, late):
            return yg[:, late, :, :] if u == 0 else b2b[:, 1 + 4 * late:5 + 4 * late, :]
        base_o = yg[:, 1, :, :].rearrange("p (q h) c -> p q (h c)", q=2)
        base_c = stage[:, :, 2 * C:4 * C]
        bob = yg[:, 0, 0, :]

        scratch = Wt[:, SCR:NCH, :, :].rearrange("p a s n -> p (a s n)")
        at = [0]

        def carve(shape, dt, parts=P):
            n = 1
            for d in shape:
                n *= d
            words = n * (1 if dt == f16 else 2)
            ap = scratch[0:parts, at[0]:at[0] + words]
            at[0] += words + words % 2
            if dt != f16:
                ap = ap.bitcast(dt)
            if len(shape) == 2:
                ap = ap.rearrange("p (a b) -> p a b", b=shape[1])
            elif len(shape) == 3:
                ap = ap.rearrange("p (a b c) -> p a b c", b=shape[1], c=shape[2])
            return ap

        Wa = carve([2, 2, CHUNK], f16)
        xs = carve([2, TB * C], f32)
        xo = carve([2, TB * C], f32)
        L = carve([NG, E], f32)
        tm = carve([NT * E], f32)
        tb = carve([NG, E], f32)
        M1, M2 = carve([NG, E], f32), carve([NG, E], f32)
        cx = carve([NG + 1, E], f16)
        iota_e, iota_m = carve([NG, E], f32), carve([E, 16], f32)
        br2s = carve([E], f32)
        assert at[0] <= 8 * 2 * CHUNK
        at[0] = 8 * 2 * CHUNK
        oh = carve([4 * TB, P + COLS], f16)
        prow, pcol = carve([NG * 2], f16), carve([NG * 2], f16)
        iota_p, iota_c = carve([P], f16), carve([COLS], f16)
        tok = carve([NG * 2], f16)
        sm = carve([12, NG], f32)
        cum = carve([4, 2 * E], f32)
        iota_j, ej = carve([NT, E], f32, 1), carve([2, NT], f32, 1)
        posf, pint = carve([NG, 2], f32), carve([3, NG * 2], i32)
        before, ones = carve([P], f16), carve([P], f16)
        ranks = carve([NG + 1, E], f32)
        assert at[0] <= (NCH - SCR) * 2 * CHUNK
        ta = tm[:, 0:NG * E].rearrange("p (g e) -> p g e", e=E)
        cmp_m = tm[:, 0:E * 16].rearrange("p (e m) -> p e m", m=16)
        cmp_j = tm[0:1, 0:NT * E].rearrange("p (j e) -> p j e", e=E)

        bank = [ctx.enter_context(nc.psum_tensor(f"bank{i}", [P, 512], f32)) for i in range(8)]
        Q_B = (0, 1)
        KV_B = (2, 3)
        KT_B = 4
        KO_B = (5, 6)
        N_B = 7
        T_B, R_B = Q_B
        UP_B = (2, 3, 5, 6)
        Y_B = (4, 7)

        def bank16(i):
            return bank[i][:, :].bitcast(f16)

        consts_up, small_in, b2_in, bsum_done = sem("consts_up"), sem("small_in"), sem("b2_in"), sem("bsum_done")
        w_in, wo_in, w_hi, w_lo = sem2("weight_loaded"), sem2("opening_weight_loaded"), sem("weight_hi_done"), sem("weight_lo_done")
        wr_hi, wr_lo = sem("router_weight_hi"), sem("router_weight_lo")
        x_in, xo_in, rows_st, base_st = sem2("x_loaded"), sem2("x_again_loaded"), sem2("rows_stored"), sem2("base_stored")
        stats_d, aggr_d, var_d, sd_d = sem("bn_stats_done"), sem("mean_var_step"), sem("var_done"), sem("std_done")
        nw_d, xn_d, xhi_d, xlo_d = sem("newton_step"), sem("normed_done"), sem("normed_hi_done"), sem("normed_lo_done")
        tr_d, xth_d, xtl_d = sem("transposed"), sem("xT_hi_done"), sem("xT_lo_done")
        hid_d, r_d, lg_ps, lg_d = sem("router_hidden_done"), sem("router_relu_done"), sem("logits_product"), sem("logits_done")
        q_ps, qr_d, q_hi, q_lo = sem("q_product"), sem("q_relu_done"), sem("q_hi_done"), sem("q_lo_done")
        kv_ps, kr_d, kv_hi, kv_lo = sem("kv_product"), sem("k_relu_done"), sem("kv_hi_done"), sem("kv_lo_done")
        kt_ps, kt_hi, kt_lo = sem("kvT_product"), sem("kvT_hi_done"), sem("kvT_lo_done")
        ko_ps, ko_hi, ko_lo = sem("kvo_product"), sem("kvo_hi_done"), sem("kvo_lo_done")
        n_ps, n_d, den_d, z_d = sem("num_product"), sem("attended"), sem("den_done"), sem("z_done")
        chain, rexp, dif_d, cx_d = sem("route_step"), sem("route_exp"), sem("route_dif"), sem("chosen_done")
        rank_d, rank_read, route_d = sem("rank_done"), sem("rank_read"), sem("route_done")
        eq_d, oh_d, tab_ps, list_d = sem("columns_compared"), sem("one_hots_done"), sem("list_product"), sem("list_done")
        xo_rows, xg_in = sem2("opening_rows_in"), sem2("tile_rows_in")
        idx_d, tr3_d, xt_d = sem("gather_rows_done"), sem("tile_transposed"), sem("tile_T_done")
        up_ps, h_d, h_hi, h_lo = sem("up_product"), sem("silu_done"), sem("hidden_hi_done"), sem("hidden_lo_done")
        y_ps, y_ev, y_st = sem("down_product"), sem("down_evacuated"), sem2("y_stored")
        bs_in, bs_d = sem2("base_rows_in"), sem("base_added")
        idy_d, yg_in, cb, cb_d = sem2("gather_places_done"), sem2("expert_rows_in_even") + sem2("expert_rows_in_odd"), sem("combine_step"), sem("combined")
        lt_in, lt, lt_d, lt_st = sem2("late_base_in"), sem("late_step"), sem("late_combined"), sem2("late_stored")

        block = ctx.enter_context(nc.Block())

        def chunk_of(c, part):
            return Wt[:, ds(c, 1), part, :].rearrange("p a n -> p (a n)")

        @block.sync
        def _(sp):
            def batch(v, b):
                return v[ds(b, 1)].rearrange("a p n -> (a p) n")

            def shared(v, g, u):
                return v[u, ds(g, 1)].rearrange("a p n -> (a p) n")

            for b in range(2):
                sp.dma_start(xs[:, b, :], x_v[b]).then_inc(x_in[b], 16)
            for dst, src in ((Wrf[:, :, :], wr), (wr2s[:, :], wr2), (br1s[:, :], br1), (b1s[:, :], b1),
                             (br2s, br2.to_broadcast([P, E]))):
                sp.dma_start(dst, src).then_inc(small_in, 16)
            for b in range(2):
                sp.dma_start(xo[:, b, :], x_v[b]).then_inc(xo_in[b], 16)

            def rows_out(b, q):
                sp.wait_ge(xlo_d, b + 1)
                sp.dma_start(batch(rows_v, b), xhl[:, q, :, :, :].rearrange("p t s c -> p (t s c)")).then_inc(rows_st[q], 16)

            def x_load(b, q):
                sp.wait_ge(xn_d, b - 1)
                sp.dma_start(xs[:, q, :], batch(x_v, b)).then_inc(x_in[q], 16)

            def base_out(b, q):
                sp.wait_ge(n_d, b * 4 + 8)
                sp.dma_start(batch(base_v, b), xo[:, q, :]).then_inc(base_st[q], 16)

            def xo_load(b, q, g):
                sp.wait_ge(base_st[q], g * 16 + 16)
                sp.dma_start(xo[:, q, :], batch(x_v, b)).then_inc(xo_in[q], 16)

            for b in range(2):
                rows_out(b, b)
                x_load(b + 2, b)
            with sp.Fori(0, NB // 2 - 2) as g:
                for q in range(2):
                    b = g * 2 + q
                    rows_out(b + 2, q)
                    x_load(b + 4, q)
                    base_out(b, q)
                    xo_load(b + 2, q, g)
            for b in (NB - 4, NB - 3):
                rows_out(b + 2, b % 2)
                base_out(b, b % 2)
                xo_load(b + 2, b % 2, b // 2)
            for u in range(2):
                sp.wait_ge(rows_st[u], 2 * 16)
            for u in range(2):
                sp.dma_start(xg[:, u, :, :].rearrange("p h n -> p (h n)"), rows_s[u, 0]).then_inc(xo_rows[u], 16)
            for b in (NB - 2, NB - 1):
                base_out(b, b % 2)
            def chunks(J):
                for i in range(2):
                    sp.wait_ge(w_lo, J * 2 + (CH_OPEN + 1 + i))
                    sp.dma_start(stage[:, i, :], wts[ds(J * 2 + (CH_OPEN + i), 1)].rearrange("a p n -> (a p) n")).then_inc(wo_in[i], 16)

            def opening(g, q, ahead, chunks_ahead=True, first=False):
                J = g * 2 + q
                if ahead:
                    sp.wait_ge(tr3_d, J + 3)
                    sp.dma_start(xg[:, q, :, :].rearrange("p h n -> p (h n)"), shared(rows_s, g + 1, q)).then_inc(xo_rows[q], 16)
                sp.wait_ge(bs_d, J + 1)
                sp.wait_ge(base_st[0], NB // 2 * 16)
                sp.wait_ge(base_st[1], NB // 2 * 16)
                sp.dma_start(base_o[:, q, :], shared(base_s, g, q)).then_inc(bs_in[q], 16)
                if first:
                    chunks(0)
                    sp.dma_start(b2b[:, :, :].rearrange("p e c -> p (e c)"),
                                 b2.to_broadcast([P, (E + 1) * C])).then_inc(b2_in, 16)
                    sp.dma_start(bob, bo.to_broadcast([P, C])).then_inc(b2_in, 16)
                if chunks_ahead:
                    chunks(J + 1)
                sp.wait_ge(bs_d, J + 3)
                sp.dma_start(shared(base_s, g, q), ysb[:, q, :]).then_inc(y_st[q], 16)
            opening(0, 0, True, first=True)
            opening(0, 1, True)
            with sp.Fori(1, N1 // 2 - 1) as g:
                for q in range(2):
                    opening(g, q, True)
            for q in range(2):
                opening(N1 // 2 - 1, q, False, q == 0)

            def y_out(g, q):
                j = g * 2 + q
                sp.wait_ge(y_ev, j + (N1 + 3))
                sp.dma_start(ys_v[ds(j, 1)].rearrange("a p n -> (a p) n"), ysb[:, q, :]).then_inc(y_st[q], 16)
            with sp.Fori(0, NT // 2) as g:
                for q in range(2):
                    y_out(g, q)
            y_out(NT // 2, 0)

            def base_load(g, u):
                sp.dma_start(base_c[:, 1 - u, :], shared(base_s, g + N1 // 2, u)).then_inc(bs_in[1 - u], 16)

            def late_load(g, u):
                sp.dma_start(stage[:, u, 0:2 * C], shared(base_s, g, u)).then_inc(lt_in[u], 16)
            sp.wait_ge(w_lo, 2 + NCH)
            for u in range(2):
                sp.wait_ge(y_st[u], (N1 // 2 + 1) * 16)
            for u in range(2):
                base_load(0, u)
                late_load(0, u)

            def closing(g, u, ahead):
                i = g * 2 + u
                sp.wait_ge(lt_d, i + 3)
                sp.dma_start(shared(out_s, g, u), stage[:, u, 0:2 * C]).then_inc(lt_st[u], 16)
                sp.wait_ge(cb_d, i + 3)
                sp.dma_start(shared(out_s, g + N1 // 2, u), ysb[:, 1 - u, :]).then_inc(y_st[1 - u], 16)
                if ahead:
                    base_load(g + 1, u)
                    sp.wait_ge(lt_st[u], g * 16 + 16)
                    late_load(g + 1, u)
            with sp.Fori(0, N1 // 2 - 1) as g:
                for u in range(2):
                    closing(g, u, True)
            for u in range(2):
                closing(N1 // 2 - 1, u, False)
            sp.wait_ge(y_st[0], ((NALL + 1) // 2 + 1) * 16)
            sp.wait_ge(y_st[1], (NALL // 2 + 1) * 16)
            for u in range(2):
                sp.wait_ge(lt_st[u], N1 // 2 * 16)

        @block.gpsimd
        def _(pool):
            for q in range(2):
                pool.dma_start(stage[:, q, :], wa[q]).then_inc(w_in[q], 16)
            for q in range(2):
                pool.sem_inc(rows_st[q], 16)
                pool.sem_inc(y_st[q], 16)
            pool.sem_inc(n_d, 4)
            pool.sem_inc(idx_d, N1)
            pool.sem_inc(tab_ps, 1)
            for s in (tr3_d, y_ev, bs_d, cb_d, lt_d):
                pool.sem_inc(s, 2)
            pool.sem_inc(h_lo, 4)
            pool.memset(ident[:, :], 0.0)
            pool.memset(before, 1.0)
            pool.memset(ones, 1.0)
            pool.memset(cx[:, NG, :], 0.0)
            pool.memset(cum, 0.0)
            pool.memset(half[:, :], 0.5).then_inc(consts_up, 1)
            pool.wait_ge(consts_up, 1)
            pool.affine_select(out=ident[:, :], in_=ident[:, :], compare_op=ALU.not_equal, fill=1.0,
                               base=0, pattern=[[-1, P]], channel_multiplier=1).then_inc(consts_up, 1)
            pool.affine_select(out=before, in_=before, compare_op=ALU.is_gt, fill=0.0,
                               base=0, pattern=[[1, P]], channel_multiplier=-1)

            def count(dst, pattern, base=0, by_partition=0):
                return pool.iota(dst, pattern=pattern, base=base, channel_multiplier=by_partition,
                                 allow_small_or_imprecise_dtypes=True)
            count(iota_e, [[0, NG], [1, E]])
            count(iota_m, [[0, E], [TILE, 16]])
            count(iota_j, [[1, NT], [0, E]])
            count(iota_p, [[1, P]])
            count(iota_c, [[1, COLS]])
            count(tok, [[SEQ, NB], [1, TB], [0, 2]], base=-(ROWS // 2), by_partition=TB).then_inc(consts_up, 1)
            with pool.Fori(0, CH_OPEN // 2) as g:
                for q in range(2):
                    pool.wait_ge(w_lo, g * 2 + q + 1)
                    pool.dma_start(stage[:, q, :],
                                   wts[ds(g * 2 + q, 1)].rearrange("a p n -> (a p) n")).then_inc(w_in[q], 16)
            pool.wait_ge(list_d, 1)

            def gather(g, q):
                j = g * 2 + q
                pool.wait_ge(tr3_d, j + (N1 + 1))
                pool.tensor_copy(idxc[:, q, :], list_i[:, ds(j * 2, 2)]).then_inc(idx_d, 1)
                for r in range(2):
                    pool.wait_ge(rows_st[r], (NB // 2 + 1) * 16)
                pool.wait_ge(idx_d, j + (N1 + 1))
                for h in range(2):
                    pool.indirect_dma_start(
                        out=xg[:, q, h, :], out_offset=None, in_=rows_d[:, :],
                        in_offset=bass.IndirectOffsetOnAxis(ap=idxc[:, q, h:h + 1], axis=0)).then_inc(xg_in[q], 16)
            with pool.Fori(0, NT // 2) as g:
                for q in range(2):
                    gather(g, q)
            gather(NT // 2, 0)

            def shared_rows(g, u):
                pool.wait_ge(tr3_d, g * 2 + (N2 + u + 1))
                pool.dma_start(xg[:, 1 - u, :, :].rearrange("p h n -> p (h n)"),
                               rows_s[u, ds(g + N1 // 2, 1)].rearrange("a p n -> (a p) n")).then_inc(xg_in[1 - u], 32)

            def expert_rows(g, u, late):
                i = g * 2 + u
                pool.wait_ge(lt_d if late else cb_d, i + 1)
                pool.tensor_copy(idxy[:, u, late, :], pos_i[:, ds(i * 4 + (0 if late else 4 * N1), 4)]).then_inc(idy_d[late], 1)
                for r in range(2):
                    pool.wait_ge(y_st[r], ((N2 + 1 - r) // 2 + 1) * 16)
                pool.wait_ge(idy_d[late], i + 1)
                for k in range(4):
                    pool.indirect_dma_start(
                        out=gathered(u, late)[:, k, :], out_offset=None, in_=ys_d[:, :],
                        in_offset=bass.IndirectOffsetOnAxis(ap=idxy[:, u, late, k:k + 1], axis=0)).then_inc(yg_in[2 * u + late], 16)
            shared_rows(0, 0)
            shared_rows(0, 1)
            shared_rows(1, 0)

            def closing(g, u, ahead):
                expert_rows(g, u, 1)
                expert_rows(g, u, 0)
                if ahead:
                    shared_rows(g + 1 + u, 1 - u)
            with pool.Fori(0, N1 // 2 - 2) as g:
                for u in range(2):
                    closing(g, u, True)
            closing(N1 // 2 - 2, 0, True)
            closing(N1 // 2 - 2, 1, False)
            for u in range(2):
                closing(N1 // 2 - 1, u, False)

        @block.scalar
        def _(act):
            A = nc.scalar.activation

            def split_hi(q, turn, dst, loaded=w_in):
                act.wait_ge(loaded[q], turn * 16 + 16)
                A(dst, stage[:, q, :], ACT.Copy, scale=S_W).then_inc(w_hi, 1)

            def std(b, q):
                act.wait_ge(var_d, b + 1)
                A(sd[:, q, :], ve[:, q, :], ACT.Sqrt).then_inc(sd_d, 1)

            def x_hi(b, q, turn):
                act.wait_ge(xn_d, b + 1)
                act.wait_ge(rows_st[q], turn * 16 + 16)
                A(xhl[:, q, :, 0, :], xn[:, :, :], ACT.Copy).then_inc(xhi_d, 1)

            def xT_hi(b, q):
                act.wait_ge(tr_d, b * 2 + 1)
                A(xT[:, q, 0, :, :].rearrange("p c n -> p (c n)"), bank16(KV_B[0]), ACT.Copy).then_inc(xth_d, 1)

            def router(b):
                act.wait_ge(hid_d, b + 1)
                A(rr[:, :], bank[N_B][0:HID, :], ACT.Relu, bias=br1s[:, 0:1], scale=1.0 / (S_X * S_W)).then_inc(r_d, 1)

            def xT_lo(b, q):
                act.wait_ge(tr_d, b * 2 + 2)
                A(xT[:, q, 1, :, :].rearrange("p c n -> p (c n)"), bank16(KV_B[1]), ACT.Copy).then_inc(xtl_d, 1)

            def q_part(b, h):
                act.wait_ge(q_ps, b * 2 + h + 1)
                A(qr[:, h, :], bank[Q_B[h]][:, :], ACT.Relu, scale=SC).then_inc(qr_d, 1)
                act.wait_ge(qr_d, b * 2 + h + 1)
                A(qs[:, 0, h, :], qr[:, h, :], ACT.Copy, bias=EPS * S_Q).then_inc(q_hi, 1)

            def kv_part(b, t):
                act.wait_ge(kv_ps, b * 4 + t + 1)
                A(kr[:, t % 2, :], bank[KV_B[t % 2]][:, 0:C], ACT.Relu, scale=SC).then_inc(kr_d, 1)
                A(vs[:, 0, t, :], bank[KV_B[t % 2]][:, C:2 * C], ACT.Copy, scale=SC)
                act.wait_ge(kr_d, b * 4 + t + 1)
                A(ks[:, 0, t, :], kr[:, t % 2, :], ACT.Copy, bias=EPS * S_Q).then_inc(kv_hi, 1)

            def kvT_hi(b):
                act.wait_ge(kt_ps, b + 1)
                A(kvT[:, 0, :, :], bank[KT_B][:, :].rearrange("p (h d) -> p h d", h=2), ACT.Copy,
                  scale=S_KV / (S_Q * S_Q)).then_inc(kt_hi, 1)

            def kvo_hi(b):
                act.wait_ge(ko_ps, b + 1)
                for h in range(2):
                    ins = A(kvo[:, 0, h, 0:C + 1], bank[KO_B[h]][:, 0:C + 1], ACT.Copy, scale=1.0 / S_W)
                ins.then_inc(ko_hi, 1)

            def rows_T(J, q):
                act.wait_ge(tr3_d, J + 3)
                A(xt[:, q, :, :].rearrange("p s n -> p (s n)"), bank16(T_B), ACT.Copy).then_inc(xt_d, 1)

            def chunk(b, i):
                split_hi(i % 2, b + (1 + i // 2), chunk_of(b * 2 + i, 0))

            def batch(b, q, g):
                kvT_hi(b)
                router(b + 1)
                std(b + 2, q)
                kv_part(b + 1, 0)
                kvo_hi(b)
                kv_part(b + 1, 1)
                x_hi(b + 2, q, g + 1)
                kv_part(b + 1, 2)
                chunk(b, 0)
                kv_part(b + 1, 3)
                chunk(b, 1)
                q_part(b + 1, 0)
                xT_hi(b + 2, q)
                xT_lo(b + 2, q)
                q_part(b + 1, 1)

            act.preload_act_table(ACT.Sqrt)
            std(0, 0)
            act.wait_ge(small_in, 80)
            A(Wr[:, 0, :, :], Wrf[:, :, :], ACT.Copy, scale=S_W).then_inc(wr_hi, 1)
            x_hi(0, 0, 0)
            for q in range(2):
                split_hi(q, 0, Wa[:, q, 0, :])
            xT_hi(0, 0)
            xT_lo(0, 0)
            std(1, 1)
            router(0)
            for t in range(TB):
                kv_part(0, t)
                if t == 1:
                    x_hi(1, 1, 0)
            q_part(0, 0)
            xT_hi(1, 1)
            xT_lo(1, 1)
            q_part(0, 1)
            with act.Fori(0, NB // 2 - 1) as g:
                for q in range(2):
                    batch(g * 2 + q, q, g)
            b = NB - 2
            kvT_hi(b)
            router(b + 1)
            kv_part(b + 1, 0)
            kvo_hi(b)
            kv_part(b + 1, 1)
            chunk(b, 0)
            kv_part(b + 1, 2)
            chunk(b, 1)
            kv_part(b + 1, 3)
            for h in range(2):
                q_part(b + 1, h)
            chunk(b, 2)
            b = NB - 1
            kvT_hi(b)
            chunk(b, 1)
            rows_T(0, 0)
            kvo_hi(b)
            chunk(b, 2)
            rows_T(1, 1)
            act.preload_act_table(ACT.Silu)
            chunk(b, 3)

            def silus(J, q, eb):
                for k in range(5):
                    if k < 4:
                        act.wait_ge(up_ps, J * 4 + k + 1)
                        act.wait_ge(h_lo, J * 4 + k + 1)
                        for i in range(2):
                            ins = A(hb[:, k, i * TILE:(i + 1) * TILE], bank[UP_B[k]][:, i * TILE:(i + 1) * TILE], ACT.Silu,
                                    bias=b1s[:, ds(eb + (2 * k + i), 1)], scale=1.0 / (S_X * S_W))
                        ins.then_inc(h_d, 1)
                    if k > 0:
                        act.wait_ge(h_d, J * 4 + k)
                        A(hs[:, q, 0, 2 * k - 2:2 * k, :].rearrange("p i n -> p (i n)"), hb[:, k - 1, :],
                          ACT.Copy, scale=S_H).then_inc(h_hi, 1)

            def opening(g, q):
                J = g * 2 + q
                silus(J + 1, 1 - q, 0)
                opening_chunks(J)
                rows_T(J + 2, q)

            def opening_chunks(J):
                for i in range(2):
                    split_hi(i, J, chunk_of(J * 2 + (CH_OPEN + i), 0), wo_in)

            act.wait_ge(n_d, NB * 4 + 4)
            silus(0, 0, 0)
            for i in (4, 5):
                chunk(b, i)
            silus(1, 1, 0)
            rows_T(2, 0)
            act.preload_act_table(ACT.Exp)
            act.wait_ge(dif_d, 1)
            A(tb, tb, ACT.Exp).then_inc(rexp, 1)
            A(sm[:, 5, :], sm[:, 4, :], ACT.Exp).then_inc(rexp, 1)
            act.wait_ge(dif_d, 2)
            A(sm[:, 9, :], sm[:, 8, :], ACT.Exp, scale=0.5).then_inc(rexp, 1)
            act.preload_act_table(ACT.Silu)
            opening_chunks(0)
            opening(0, 1)
            with act.Fori(1, N1 // 2 - 1) as g:
                for q in range(2):
                    opening(g, q)
            act.wait_ge(tab_ps, 5)
            opening_chunks(N1 - 2)
            silus(N1 - 1, 1, 0)
            rows_T(N1, 0)
            opening_chunks(N1 - 1)
            act.wait_ge(route_d, 1)
            silus(N1, 0, act.value_load(et[0:1, 2, 0:1], min_val=0, max_val=8 * E))
            rows_T(N1 + 1, 1)
            with act.Fori(0, NT // 2) as g:
                for q in range(2):
                    j = g * 2 + (1 + q)
                    silus(j + N1, 1 - q, act.value_load(et[0:1, 2, ds(j, 1)], min_val=0, max_val=8 * E))
                    rows_T(j + (N1 + 1), q)
            with act.Fori(0, N1 // 2 - 1) as g:
                for u in range(2):
                    silus(g * 2 + (N2 + u), 1 - u, 0)
                    rows_T(g * 2 + (N2 + 1 + u), u)
            silus(NALL - 2, 1, 0)
            rows_T(NALL - 1, 0)
            silus(NALL - 1, 0, 0)

        @block.vector
        def _(dve):
            V = nc.vector
            steps = [0]

            def link(ins):
                steps[0] += 1
                ins.then_inc(chain, 1)
                dve.wait_ge(chain, steps[0])

            def split_lo(n, q, hi, lo):
                dve.wait_ge(w_hi, n + 1)
                V.scalar_tensor_tensor(out=lo, in0=stage[:, q, :], scalar=S_W, in1=hi,
                                       op0=ALU.mult, op1=ALU.subtract).then_inc(w_lo, 1)

            def chunk(b, i):
                c = b * 2 + i
                split_lo(c + 2, i % 2, chunk_of(c, 0), chunk_of(c, 1))

            def stats(b, q, turn):
                dve.wait_ge(x_in[q], turn * 16 + 16)
                for t in range(TB):
                    ins = V.bn_stats(st[:, q, t, :], xs[:, q, t * C:(t + 1) * C])
                ins.then_inc(stats_d, 1)

            def variance(b, q):
                dve.wait_ge(stats_d, b + 1)
                m0, v0, m1, v1 = (st[:, q, :, k] for k in (1, 2, 4, 5))
                V.tensor_tensor(mv[:, 0, :], m0, m1, ALU.add)
                V.tensor_tensor(mv[:, 1, :], m0, m1, ALU.subtract)
                V.tensor_tensor(mv[:, 2, :], v0, v1, ALU.add).then_inc(aggr_d, 1)
                dve.wait_ge(aggr_d, b * 2 + 1)
                V.tensor_scalar(mu[:, q, :], mv[:, 0, :], 0.5, None, ALU.mult)
                V.tensor_tensor(mv[:, 3, :], mv[:, 1, :], mv[:, 1, :], ALU.mult)
                V.tensor_scalar(mv[:, 4, :], mv[:, 2, :], 1.0 / C, LN_EPS, ALU.mult, ALU.add).then_inc(aggr_d, 1)
                dve.wait_ge(aggr_d, b * 2 + 2)
                V.scalar_tensor_tensor(out=ve[:, q, :], in0=mv[:, 3, :], scalar=0.25, in1=mv[:, 4, :],
                                       op0=ALU.mult, op1=ALU.add).then_inc(var_d, 1)

            def norm(b, q, first=False):
                def step(ins, k):
                    ins.then_inc(nw_d, 1)
                    dve.wait_ge(nw_d, b * 5 + k)
                dve.wait_ge(sd_d, b + 1)
                step(V.reciprocal(nw[:, 0, :], sd[:, q, :]), 1)
                step(V.tensor_tensor(nw[:, 1, :], nw[:, 0, :], nw[:, 0, :], ALU.mult), 2)
                step(V.tensor_tensor(nw[:, 2, :], nw[:, 1, :], ve[:, q, :], ALU.mult), 3)
                step(V.tensor_scalar(nw[:, 3, :], nw[:, 2, :], -0.5 * S_X, 1.5 * S_X, ALU.mult, ALU.add), 4)
                step(V.tensor_tensor(rs[:, q, :], nw[:, 0, :], nw[:, 3, :], ALU.mult), 5)
                if not first:
                    dve.wait_ge(xlo_d, b)
                for t in range(TB):
                    ins = V.tensor_scalar(xn[:, t, :], xs[:, q, t * C:(t + 1) * C], mu[:, q, t:t + 1],
                                          rs[:, q, t:t + 1], ALU.subtract, ALU.mult)
                ins.then_inc(xn_d, 1)

            def x_lo(b, q):
                dve.wait_ge(xhi_d, b + 1)
                V.tensor_tensor(xhl[:, q, :, 1, :], xn[:, :, :], xhl[:, q, :, 0, :], ALU.subtract).then_inc(xlo_d, 1)

            def logits(b):
                dve.wait_ge(lg_ps, b + 1)
                V.tensor_tensor(L[:, ds(b * TB, TB), :], bank[N_B][:, 0:TB * E].rearrange("p (t e) -> p t e", e=E),
                                br2s.rearrange("p (a e) -> p a e", a=1).to_broadcast([P, TB, E]), ALU.add).then_inc(lg_d, 1)

            def q_part(b, h):
                dve.wait_ge(q_hi, b * 2 + h + 1)
                V.scalar_tensor_tensor(out=qs[:, 1, h, :], in0=qr[:, h, :], scalar=EPS * S_Q, in1=qs[:, 0, h, :],
                                       op0=ALU.add, op1=ALU.subtract).then_inc(q_lo, 1)

            def kv_part(b, t):
                dve.wait_ge(kv_hi, b * 4 + t + 1)
                V.scalar_tensor_tensor(out=vs[:, 1, t, :], in0=bank[KV_B[t % 2]][:, C:2 * C], scalar=SC, in1=vs[:, 0, t, :],
                                       op0=ALU.mult, op1=ALU.subtract)
                V.scalar_tensor_tensor(out=ks[:, 1, t, :], in0=kr[:, t % 2, :], scalar=EPS * S_Q, in1=ks[:, 0, t, :],
                                       op0=ALU.add, op1=ALU.subtract).then_inc(kv_lo, 1)

            def kvT_lo(b):
                dve.wait_ge(kt_hi, b + 1)
                V.scalar_tensor_tensor(out=kvT[:, 1, :, :], in0=bank[KT_B][:, :].rearrange("p (h d) -> p h d", h=2),
                                       scalar=S_KV / (S_Q * S_Q), in1=kvT[:, 0, :, :],
                                       op0=ALU.mult, op1=ALU.subtract).then_inc(kt_lo, 1)

            def kvo_lo(b):
                dve.wait_ge(ko_hi, b + 1)
                for h in range(2):
                    ins = V.scalar_tensor_tensor(out=kvo[:, 1, h, 0:C + 1], in0=bank[KO_B[h]][:, 0:C + 1], scalar=1.0 / S_W,
                                                 in1=kvo[:, 0, h, 0:C + 1], op0=ALU.mult, op1=ALU.subtract)
                ins.then_inc(ko_lo, 1)

            def attend(b, q, turn, tiles=range(TB)):
                if tiles[0] == 0:
                    dve.wait_ge(xo_in[q], turn * 16 + 16)
                for t in tiles:
                    num = bank[N_B if t % 2 == 0 else KT_B]
                    dve.wait_ge(n_ps, b * 4 + t + 1)
                    V.tensor_scalar_add(zz[:, 0, t:t + 1], num[:, C:C + 1], EPS * S_Q * S_KV).then_inc(den_d, 1)
                    dve.wait_ge(den_d, b * 4 + t + 1)
                    V.reciprocal(zz[:, 1, t:t + 1], zz[:, 0, t:t + 1]).then_inc(z_d, 1)
                    dve.wait_ge(z_d, b * 4 + t + 1)
                    V.scalar_tensor_tensor(out=xo[:, q, t * C:(t + 1) * C], in0=num[:, 0:C], scalar=zz[:, 1, t:t + 1],
                                           in1=xo[:, q, t * C:(t + 1) * C], op0=ALU.mult, op1=ALU.add).then_inc(n_d, 1)

            def batch(b, q, g):
                stats(b + 2, q, g + 1)
                kvT_lo(b)
                variance(b + 2, q)
                norm(b + 2, q)
                kv_part(b + 1, 0)
                kvo_lo(b)
                kv_part(b + 1, 1)
                logits(b + 1)
                x_lo(b + 2, q)
                kv_part(b + 1, 2)
                attend(b, q, g, (0, 1))
                kv_part(b + 1, 3)
                attend(b, q, g, (2, 3))
                chunk(b, 0)
                q_part(b + 1, 0)
                chunk(b, 1)
                q_part(b + 1, 1)

            stats(0, 0, 0)
            variance(0, 0)
            norm(0, 0, first=True)
            dve.wait_ge(wr_hi, 1)
            V.scalar_tensor_tensor(out=Wr[:, 1, :, :], in0=Wrf[:, :, :], scalar=S_W, in1=Wr[:, 0, :, :],
                                   op0=ALU.mult, op1=ALU.subtract).then_inc(wr_lo, 1)
            x_lo(0, 0)
            for q in range(2):
                split_lo(q, q, Wa[:, q, 0, :], Wa[:, q, 1, :])
            stats(1, 1, 0)
            variance(1, 1)
            norm(1, 1)
            logits(0)
            for t in range(TB):
                kv_part(0, t)
                if t == 1:
                    x_lo(1, 1)
            for h in range(2):
                q_part(0, h)
            with dve.Fori(0, NB // 2 - 1) as g:
                for q in range(2):
                    batch(g * 2 + q, q, g)
            b = NB - 2
            kvT_lo(b)
            kv_part(b + 1, 0)
            kvo_lo(b)
            kv_part(b + 1, 1)
            logits(b + 1)
            kv_part(b + 1, 2)
            chunk(b, 0)
            attend(b, 0, b // 2, (0, 1))
            kv_part(b + 1, 3)
            attend(b, 0, b // 2, (2, 3))
            chunk(b, 1)
            for h in range(2):
                q_part(b + 1, h)
            chunk(b, 2)
            b = NB - 1
            kvT_lo(b)
            chunk(b, 1)
            kvo_lo(b)
            chunk(b, 2)
            attend(b, 1, b // 2)
            chunk(b, 3)

            def over_e(small):
                return small.rearrange("p (g a) -> p g a", a=1).to_broadcast([P, NG, E])
            m1, a1, m2, a2, d2, x2, z, g2, dd, uu, den, tmp = (sm[:, k, :] for k in range(12))

            def choose(best, mask, first_at):
                link(V.tensor_reduce(best, L, AX.X, ALU.max))
                link(V.tensor_tensor(ta, L, over_e(best), ALU.is_equal))
                link(V.scalar_tensor_tensor(out=ta, in0=ta, scalar=-float(E), in1=iota_e, op0=ALU.mult, op1=ALU.add))
                link(V.tensor_reduce(first_at, ta, AX.X, ALU.min))
                link(V.tensor_tensor(mask, ta, over_e(first_at), ALU.is_equal))

            def choices():
                dve.wait_ge(lg_d, NB)
                dve.wait_ge(consts_up, 3)
                choose(m1, M1, a1)
                link(V.tensor_tensor(tb, L, over_e(m1), ALU.subtract))
                link(V.scalar_tensor_tensor(out=L, in0=M1, scalar=-1e30, in1=L, op0=ALU.mult, op1=ALU.add))
                choose(m2, M2, a2)
                V.tensor_tensor(d2, m2, m1, ALU.subtract).then_inc(dif_d, 1)
                V.tensor_tensor(cx[:, 0:NG, :], M1, M2, ALU.add).then_inc(cx_d, 1)

            def gates():
                dve.wait_ge(rexp, 2)
                link(V.tensor_reduce(tmp, tb, AX.X, ALU.add))
                link(V.reciprocal(z, tmp))
                link(V.tensor_tensor(g2, x2, z, ALU.mult))
                V.tensor_tensor(dd, g2, z, ALU.subtract).then_inc(dif_d, 1)
                dve.wait_ge(rexp, 3)
                link(V.tensor_scalar_add(den, uu, 1.0))
                link(V.reciprocal(wc[:, :, 0], den))
                link(V.tensor_tensor(wc[:, :, 1], uu, wc[:, :, 0], ALU.mult))

            def places():
                link(V.tensor_tensor(cmp_m, ranks[:, NG, :].rearrange("p (e a) -> p e a", a=1).to_broadcast([P, E, 16]),
                                     iota_m, ALU.is_gt))
                link(V.tensor_reduce(cum[:, 0, E:2 * E], cmp_m, AX.X, ALU.add))
                for k, (s, d) in zip((1, 2, 4), ((0, 1), (1, 2), (2, 0))):
                    link(V.tensor_tensor(cum[:, d, E:2 * E], cum[:, s, E:2 * E], cum[:, s, E - k:2 * E - k], ALU.add))
                link(V.tensor_tensor(cmp_j, iota_j,
                                     cum[0:1, 0, E:2 * E].rearrange("p (a e) -> p a e", a=1).to_broadcast([1, NT, E]), ALU.is_ge))
                link(V.tensor_reduce(ej[:, 0, :], cmp_j, AX.X, ALU.add))
                link(V.tensor_scalar_min(ej[:, 1, :], ej[:, 0, :], float(E - 1)))
                for k, by in enumerate((1, CE, 8)):
                    link(V.tensor_scalar(et[:, k, 0:NT], ej[:, 1, :], float(by), float(by), ALU.mult, ALU.add))
                link(V.scalar_tensor_tensor(out=tb, scalar=float(TILE), in1=ranks[:, 0:NG, :],
                                            in0=cum[:, 0, E - 1:2 * E - 1].rearrange("p (a e) -> p a e", a=1).to_broadcast([P, NG, E]),
                                            op0=ALU.mult, op1=ALU.add))
                for s, mask in enumerate((M1, M2)):
                    link(V.tensor_tensor(ta, mask, tb, ALU.mult))
                    link(V.tensor_reduce(posf[:, :, s], ta, AX.X, ALU.add))
                link(V.tensor_copy(pos_i[:, :], posf.rearrange("p g s -> p (g s)")))
                link(V.tensor_scalar(pint[:, 0, :], pos_i[:, :], 1, P - 1, ALU.logical_shift_right, ALU.bitwise_and))
                link(V.tensor_scalar(pint[:, 1, :], pos_i[:, :], 8, 1, ALU.logical_shift_right, ALU.logical_shift_left))
                link(V.tensor_scalar(pint[:, 2, :], pos_i[:, :], 1, None, ALU.bitwise_and))
                link(V.tensor_copy(prow, pint[:, 0, :]))
                V.tensor_tensor(pcol, pint[:, 1, :], pint[:, 2, :], ALU.add).then_inc(route_d, 1)

            def one_hots(m):
                dve.wait_ge(tab_ps, m + 1)
                at_m = ds(m * (4 * TB), 4 * TB)

                def ramp(r, n):
                    return r.rearrange("p (a n) -> p a n", a=1).to_broadcast([P, 4 * TB, n])

                def pairs(v, n):
                    return v[:, at_m].rearrange("p (k a) -> p k a", a=1).to_broadcast([P, 4 * TB, n])
                V.tensor_tensor(oh[:, :, P:], ramp(iota_c, COLS), pairs(pcol, COLS), ALU.is_equal).then_inc(eq_d, 1)
                V.tensor_tensor(oh[:, :, 0:P], ramp(iota_p, P), pairs(prow, P), ALU.is_equal)
                dve.wait_ge(eq_d, m + 1)
                V.tensor_tensor(oh[:, :, P:], oh[:, :, P:], pairs(tok, COLS), ALU.mult).then_inc(oh_d, 1)

            def h_parts(J, q):
                for k in range(4):
                    dve.wait_ge(h_hi, J * 4 + k + 1)
                    V.scalar_tensor_tensor(out=hs[:, q, 1, 2 * k:2 * k + 2, :].rearrange("p i n -> p (i n)"), in0=hb[:, k, :],
                                           scalar=S_H, in1=hs[:, q, 0, 2 * k:2 * k + 2, :].rearrange("p i n -> p (i n)"),
                                           op0=ALU.mult, op1=ALU.subtract).then_inc(h_lo, 1)

            def y_rows(J, q, turn, b2_row):
                dve.wait_ge(y_ps, J + 1)
                dve.wait_ge(y_st[q], turn * 16 + 16)
                V.scalar_tensor_tensor(out=ysb[:, q, :].rearrange("p (h c) -> p h c", h=2),
                                       in0=bank[Y_B[q]][:, :].rearrange("p (h c) -> p h c", h=2),
                                       scalar=1.0 / (S_H * S_W), in1=b2_row.to_broadcast([P, 2, C]),
                                       op0=ALU.mult, op1=ALU.add).then_inc(y_ev, 1)

            def add_base(J, q, bs_turn, base):
                dve.wait_ge(y_ev, J + 3)
                dve.wait_ge(bs_in[q], bs_turn * 16 + 16)
                V.tensor_tensor(ysb[:, q, :], ysb[:, q, :], base[:, q, :], ALU.add).then_inc(bs_d, 1)

            def chunks(J):
                for i in range(2):
                    c = J * 2 + (CH_OPEN + i)
                    split_lo(c + 2, i, chunk_of(c, 0), chunk_of(c, 1))

            def opening(g, q, listing=None, chunks_after=True):
                J = g * 2 + q
                h_parts(J + 1, 1 - q)
                if chunks_after:
                    chunks(J)
                if listing is not None:
                    one_hots(listing)
                y_rows(J, q, g, b2b[:, 0:1, :])
                add_base(J, q, g, base_o)

            h_parts(0, 0)
            for i in (4, 5):
                chunk(b, i)
            choices()
            h_parts(1, 1)
            gates()
            dve.wait_ge(b2_in, 32)
            V.tensor_tensor(b2b[:, 0, :], b2b[:, 0, :], bob, ALU.add).then_inc(bsum_done, 1)
            dve.wait_ge(bsum_done, 1)
            y_rows(0, 0, 0, b2b[:, 0:1, :])
            add_base(0, 0, 0, base_o)
            chunks(0)
            h_parts(2, 0)
            dve.wait_ge(rank_d, 1)
            V.tensor_copy(ranks.rearrange("p g e -> p (g e)"), bank[R_B][:, 0:(NG + 1) * E]).then_inc(rank_read, 1)
            dve.wait_ge(rank_read, 1)
            chunks(1)
            places()
            dve.wait_ge(route_d, 1)
            y_rows(1, 1, 0, b2b[:, 0:1, :])
            add_base(1, 1, 0, base_o)
            with dve.Fori(1, N1 // 2 - 1) as g:
                for q in range(2):
                    opening(g, q, listing=g * 2 + (q - 2))
            dve.wait_ge(tab_ps, 5)
            V.tensor_scalar_add(list_i[:, :], bank[R_B][:, 0:COLS], float(ROWS // 2)).then_inc(list_d, 1)
            chunks(N1 - 2)
            opening(N1 // 2 - 1, 0, chunks_after=False)
            chunks(N1 - 1)
            opening(N1 // 2 - 1, 1, chunks_after=False)

            def expert_tile(g, q):
                j = g * 2 + q
                h_parts(j + (N1 + 1), 1 - q)
                ev = dve.value_load(et[0:1, 0, ds(j, 1)], min_val=0, max_val=E)
                y_rows(j + N1, q, g + N1 // 2, b2b[:, ds(ev, 1), :])
            with dve.Fori(0, NT // 2) as g:
                for q in range(2):
                    expert_tile(g, q)
            expert_tile(NT // 2, 0)

            def weigh(dst, u, late, f4, s):
                for h in range(2):
                    half_row = dst[:, h * C:(h + 1) * C]
                    ins = V.scalar_tensor_tensor(out=half_row, in0=gathered(u, late)[:, 2 * h + s, :],
                                                 scalar=wc[:, :, :].rearrange("p g s -> p (g s)")[:, ds(f4 + (2 * h + s), 1)],
                                                 in1=half_row, op0=ALU.mult, op1=ALU.add)
                return ins

            def closing(g, u, ahead):
                q = 1 - u
                i = g * 2 + u
                J = g * 2 + (N2 + u)
                if ahead:
                    h_parts(J + 1, 1 - q)
                dve.wait_ge(lt_in[u], g * 16 + 16)
                dve.wait_ge(yg_in[2 * u + 1], g * 64 + 64)
                weigh(stage[:, u, 0:2 * C], u, 1, i * 4, 0).then_inc(lt, 1)
                dve.wait_ge(lt, i + 1)
                weigh(stage[:, u, 0:2 * C], u, 1, i * 4, 1).then_inc(lt_d, 1)
                y_rows(J, q, g + (N2 + u) // 2, b2b[:, 0:1, :])
                add_base(J, q, g + N1 // 2, base_c)
                dve.wait_ge(bs_d, i + (N1 + 3))
                dve.wait_ge(yg_in[2 * u], g * 64 + 64)
                weigh(ysb[:, q, :], u, 0, i * 4 + 4 * N1, 0).then_inc(cb, 1)
                dve.wait_ge(cb, i + 1)
                weigh(ysb[:, q, :], u, 0, i * 4 + 4 * N1, 1).then_inc(cb_d, 1)
            with dve.Fori(0, N1 // 2 - 1) as g:
                for u in range(2):
                    closing(g, u, True)
            closing(N1 // 2 - 1, 0, True)
            closing(N1 // 2 - 1, 1, False)

        @block.tensor
        def _(pe):
            mm = nc.tensor.matmul
            cam = [(c, a, m) for c in range(2) for a, m in THREE]

            def transposes(b, q):
                pe.wait_ge(xlo_d, b + 1)
                for s in range(2):
                    for c in range(2):
                        for t in range(TB):
                            ins = nc.tensor.transpose(bank16(KV_B[s])[:, c * SEQ + t * P:c * SEQ + (t + 1) * P],
                                                      xhl[:, q, t, s, c * P:(c + 1) * P], ident[:, :])
                    ins.then_inc(tr_d, 1)

            def router_hidden(b, q):
                pe.wait_ge(xth_d, b + 1)
                pe.wait_ge(xtl_d, b + 1)
                for n, (c, a, m) in enumerate(cam):
                    ins = mm(bank[N_B][0:HID, :], Wr[:, a, c, :], xT[:, q, m, c, :], start=(n == 0), stop=(n == 5))
                ins.then_inc(hid_d, 1)

            def router_logits(b):
                pe.wait_ge(r_d, b + 1)
                for t in range(TB):
                    ins = mm(bank[N_B][:, t * E:(t + 1) * E], rr[:, t * P:(t + 1) * P], wr2s[:, :], start=True, stop=True)
                ins.then_inc(lg_ps, 1)

            def q_product(b, q, halves=(0, 1)):
                for h in halves:
                    for n, (c, a, m) in enumerate(cam):
                        ins = mm(bank[Q_B[h]][:, :], Wa[:, c, a, h * P:(h + 1) * P], xT[:, q, m, c, :],
                                 start=(n == 0), stop=(n == 5))
                    ins.then_inc(q_ps, 1)

            def kv_product(b, q, tiles=range(TB)):
                for t in tiles:
                    if t >= 2:
                        pe.wait_ge(kv_lo, b * 4 + t - 1)
                    for n, (c, a, m) in enumerate(cam):
                        ins = mm(bank[KV_B[t % 2]][:, :], xT[:, q, a, c, t * P:(t + 1) * P], Wa[:, c, m, C:3 * C],
                                 start=(n == 0), stop=(n == 5))
                    ins.then_inc(kv_ps, 1)

            def kvT_product(b):
                pe.wait_ge(kv_lo, b * 4 + 4)
                pe.wait_ge(n_d, b * 4 + 4)
                for h in range(2):
                    for n, (t, a, m) in enumerate((t, a, m) for t in range(TB) for a, m in THREE):
                        ins = mm(bank[KT_B][:, h * C:(h + 1) * C], vs[:, a, t, h * P:(h + 1) * P], ks[:, m, t, :],
                                 start=(n == 0), stop=(n == 3 * TB - 1))
                ins.then_inc(kt_ps, 1)
                for h in range(2):
                    for n, (t, a) in enumerate((t, a) for t in range(TB) for a in range(2)):
                        mm(bank[KO_B[h]][:, C:C + 1], ks[:, a, t, h * P:(h + 1) * P], half[:, :],
                           start=(n == 0), stop=(n == 2 * TB - 1))

            def kvo_product(b):
                pe.wait_ge(kt_lo, b + 1)
                for h in range(2):
                    for n, (c, a, m) in enumerate(cam):
                        ins = mm(bank[KO_B[h]][:, 0:C], kvT[:, a, c, h * P:(h + 1) * P], Wa[:, c, m, 3 * C:4 * C],
                                 start=(n == 0), stop=(n == 5))
                ins.then_inc(ko_ps, 1)

            def num_product(b, tiles, logits_read):
                if tiles[0] == 0:
                    pe.wait_ge(ko_lo, b + 1)
                    pe.wait_ge(q_lo, b * 2 + 2)
                    if logits_read:
                        pe.wait_ge(lg_d, b + 2)
                for t in tiles:
                    if t >= 2:
                        pe.wait_ge(n_d, b * 4 + t + 3)
                    for n, (c, a, m) in enumerate(cam):
                        ins = mm(bank[N_B if t % 2 == 0 else KT_B][:, 0:C + 1], qs[:, a, c, t * P:(t + 1) * P],
                                 kvo[:, m, c, 0:C + 1], start=(n == 0), stop=(n == 5))
                    ins.then_inc(n_ps, 1)

            def batch(b, q, norm_ahead):
                kvT_product(b)
                router_hidden(b + 1, 1 - q)
                kv_product(b + 1, 1 - q, (0,))
                kvo_product(b)
                kv_product(b + 1, 1 - q, (1,))
                router_logits(b + 1)
                kv_product(b + 1, 1 - q, (2,))
                num_product(b, (0, 1), True)
                kv_product(b + 1, 1 - q, (3,))
                num_product(b, (2, 3), True)
                q_product(b + 1, 1 - q, (0,))
                if norm_ahead:
                    pe.wait_ge(kv_lo, b * 4 + 8)
                    transposes(b + 2, q)
                q_product(b + 1, 1 - q, (1,))

            pe.wait_ge(consts_up, 2)
            transposes(0, 0)
            pe.wait_ge(wr_lo, 1)
            router_hidden(0, 0)
            router_logits(0)
            pe.wait_ge(w_lo, 2)
            kv_product(0, 0)
            q_product(0, 0, (0,))
            pe.wait_ge(kv_lo, TB)
            transposes(1, 1)
            q_product(0, 0, (1,))
            with pe.Fori(0, NB // 2 - 1) as g:
                for q in range(2):
                    batch(g * 2 + q, q, True)
            batch(NB - 2, 0, False)

            def rows_T(J, q, turn, opening=False):
                if opening:
                    pe.wait_ge(xo_rows[q], turn * 16 + 16)
                else:
                    pe.wait_ge(xg_in[q], turn * 32 + 32)
                for s in range(4):
                    for h in range(2):
                        ins = nc.tensor.transpose(bank16(T_B)[:, s * TILE + h * P:s * TILE + (h + 1) * P],
                                                  xg[:, q, h, s * P:(s + 1) * P], ident[:, :])
                ins.then_inc(tr3_d, 1)

            def up(J, q, e4, first=False, pairs=range(4)):
                if pairs[0] == 0:
                    pe.wait_ge(xt_d, J + 1)
                for k in pairs:
                    if not first:
                        pe.wait_ge(h_d, J * 4 + (k - 3))
                    for i in range(2):
                        col = (2 * k + i) * P
                        for n, (c, a, m) in enumerate(cam):
                            ins = mm(bank[UP_B[k]][:, i * TILE:(i + 1) * TILE],
                                     Wt[:, ds(e4 + c, 1), a, col:col + P].rearrange("p a n -> p (a n)"),
                                     xt[:, q, 2 * m + c, :], start=(n == 0), stop=(n == 5))
                    ins.then_inc(up_ps, 1)

            def down(J, q, e4):
                pe.wait_ge(h_lo, J * 4 + 8)
                pe.wait_ge(y_ev, J + 1)
                for h in range(2):
                    for n, (i, a, m) in enumerate((i, a, m) for i in range(8) for a, m in THREE):
                        ins = mm(bank[Y_B[q]][:, h * C:(h + 1) * C], hs[:, q, a, i, h * P:(h + 1) * P],
                                 Wt[:, ds(e4 + (2 + i // 4), 1), m, i % 4 * C:(i % 4 + 1) * C].rearrange("p a n -> p (a n)"),
                                 start=(n == 0), stop=(n == 23))
                ins.then_inc(y_ps, 1)

            def expert_of(j):
                return pe.value_load(et[0:1, 1, ds(j, 1)], min_val=0, max_val=CE * E)

            b = NB - 1
            kvT_product(b)
            pe.wait_ge(q_hi, b * 2 + 2)
            rows_T(0, 0, 0, opening=True)
            kvo_product(b)
            pe.wait_ge(w_lo, 2 + CE)
            up(0, 0, 0, first=True, pairs=(0, 1))
            rows_T(1, 1, 0, opening=True)
            num_product(b, range(TB), False)
            up(0, 0, 0, first=True, pairs=(2, 3))

            def ranks_product():
                pe.wait_ge(cx_d, 1)
                mm(bank[R_B][:, 0:(NG + 1) * E], before, cx.rearrange("p g e -> p (g e)"), start=True, stop=False)
                for t in range(NG):
                    n = NG - t
                    ins = mm(bank[R_B][:, (t + 1) * E:(NG + 1) * E].rearrange("p (n e) -> p n e", e=E), ones,
                             cx[:, t:t + 1, :].to_broadcast([P, n, E]), start=False, stop=(t == NG - 1))
                ins.then_inc(rank_d, 1)

            def list_product(m, first=False, last=False):
                pe.wait_ge(oh_d, m + 1)
                for k in range(4 * TB):
                    ins = mm(bank[R_B][:, 0:COLS], oh[:, k, 0:P], oh[:, k, P:], start=(first and k == 0),
                             stop=(last and k == 4 * TB - 1))
                ins.then_inc(tab_ps, 1)

            def opening(J, q, turn, between=None):
                up(J + 1, 1 - q, 0)
                if between is not None:
                    between()
                rows_T(J + 2, q, turn, opening=True)
                down(J, q, 0)
            opening(0, 0, 1)
            opening(1, 1, 1, between=ranks_product)
            opening(2, 0, 2)
            opening(3, 1, 2, between=lambda: list_product(0, first=True))
            with pe.Fori(2, N1 // 2 - 1) as g:
                for q in range(2):
                    opening(g * 2 + q, q, g + 1, between=lambda: list_product(g * 2 + (q - 3)))
            list_product(3, last=True)
            up(N1 - 1, 1, 0)
            down(N1 - 2, 0, 0)
            rows_T(N1, 0, 0)
            pe.wait_ge(w_lo, 2 + NCH)
            pe.wait_ge(route_d, 1)
            up(N1, 0, expert_of(0))
            rows_T(N1 + 1, 1, 0)
            down(N1 - 1, 1, 0)
            with pe.Fori(0, NT // 2) as g:
                for q in range(2):
                    j = g * 2 + q
                    up(j + (N1 + 1), 1 - q, expert_of(j + 1))
                    rows_T(j + (N1 + 2), q, g + 1)
                    down(j + N1, q, expert_of(j))
            up(N2, 1, 0)
            rows_T(N2 + 1, 0, (N2 + 1 - N1) // 2)
            down(N2 - 1, 0, expert_of(NT - 1))
            with pe.Fori(0, N1 // 2 - 1) as g:
                for u in range(2):
                    J = g * 2 + (N2 + u)
                    up(J + 1, u, 0)
                    rows_T(J + 2, 1 - u, g + (N2 - N1 + u) // 2 + 1)
                    down(J, 1 - u, 0)
            up(NALL - 1, 0, 0)
            down(NALL - 2, 1, 0)
            down(NALL - 1, 0, 0)


def kernel(L0_attn_x, L0_attn_W_qkv, L0_attn_W_out, L0_attn_b_out, L0_ffn_Wr1, L0_ffn_br1, L0_ffn_Wr2, L0_ffn_br2,
           L0_ffn_Ws1, L0_ffn_bs1, L0_ffn_Ws2, L0_ffn_bs2, L0_ffn_We1, L0_ffn_be1, L0_ffn_We2, L0_ffn_be2):
    import numpy as np
    import concourse.bacc as bacc
    from concourse.bass_utils import run_bass_kernel_spmd

    a = {k: np.asarray(v) for k, v in dict(locals()).items() if k.startswith("L0_")}
    w1 = np.concatenate([a["L0_ffn_Ws1"][None], a["L0_ffn_We1"]])
    w2 = np.concatenate([a["L0_ffn_Ws2"][None], a["L0_ffn_We2"]])
    w1 = w1.reshape(E + 1, 2, P, I)
    w2 = w2.reshape(E + 1, 2, 4, P, C).transpose(0, 1, 3, 2, 4).reshape(E + 1, 2, P, CHUNK)
    b1 = np.concatenate([a["L0_ffn_bs1"][None], a["L0_ffn_be1"]])
    arrays = {
        "x": a["L0_attn_x"].reshape(ROWS, C),
        "wts": np.concatenate([w1, w2], 1).reshape(NCH, P, CHUNK),
        "wa": np.concatenate([a["L0_attn_W_qkv"].T, a["L0_attn_W_out"].T], 1).reshape(2, P, CHUNK),
        "wr": a["L0_ffn_Wr1"].reshape(2, P, HID).transpose(1, 0, 2),
        "br1": a["L0_ffn_br1"].reshape(HID, 1),
        "wr2": a["L0_ffn_Wr2"],
        "br2": a["L0_ffn_br2"].reshape(1, E),
        "b1": b1.reshape((E + 1) * 8, P).T,
        "b2": np.concatenate([a["L0_ffn_bs2"][None], a["L0_ffn_be2"]]).reshape(1, (E + 1) * C),
        "bo": a["L0_attn_b_out"].reshape(1, C),
    }
    arrays = {f"in_{k}": np.ascontiguousarray(v) for k, v in arrays.items()}
    nc = bacc.Bacc("TRN2", target_bir_lowering=False, num_devices=1)
    args = [nc.dram_tensor(k, v.shape, mybir.dt.from_np(v.dtype), kind="ExternalInput").ap() for k, v in arrays.items()]
    out = nc.dram_tensor("out_dram", (ROWS, C), mybir.dt.float32, kind="ExternalOutput").ap()
    build_program(nc, *args, out)
    r = run_bass_kernel_spmd(nc, [arrays], core_ids=[0])
    return r.results[0]["out_dram"].reshape(a["L0_attn_x"].shape)
```

```python
import concourse.bass as bass
from concourse import mybir
from contextlib import ExitStack

P = 128
ROWS, C, I, E = 4096, 256, 1024, 8
NB, SEQ = 8, 512
TB = SEQ // P
NG = ROWS // P
HID = C // 4
TILE = 256
NT = (2 * ROWS + E * (TILE - 1)) // TILE
NS = ROWS // TILE
N1 = NS // 2
N2 = N1 + NT
NALL = NT + NS
COLS = NT * 2
CHUNK = 1024
CE = 4
NCH = (E + 1) * CE
CH_OPEN = NCH - 2 * N1
WARM = 44
SCR = 24
S_X, S_W, S_Q, S_KV, S_H = 256.0, 256.0, 64.0, 0.125, 64.0
LN_EPS, EPS = 1e-5, 1e-6
THREE = ((0, 0), (0, 1), (1, 0))


def build_program(nc, x, wts, wa, wr, br1, wr2, br2, b1, b2, bo, out):
    f32, f16, i32 = mybir.dt.float32, mybir.dt.float16, mybir.dt.int32
    ALU, ACT, AX = mybir.AluOpType, mybir.ActivationFunctionType, mybir.AxisListType
    ds = bass.ds
    SC = S_Q / (S_X * S_W)

    rows_d = nc.dram_tensor("rows_scratch", (ROWS, 2 * C), f16).ap()
    xT_d = nc.dram_tensor("rows_T_scratch", (NB, P, 4 * SEQ), f16).ap()
    base_d = nc.dram_tensor("base_scratch", (ROWS, C), f32).ap()
    ys_d = nc.dram_tensor("expert_out_scratch", (NT * TILE, C), f32).ap()
    x_v = x.rearrange("(b p t) c -> b p (t c)", b=NB, t=TB)
    base_v = base_d.rearrange("(b p t) c -> b p (t c)", b=NB, t=TB)
    rows_v = rows_d.rearrange("(b p t) c -> b p (t c)", b=NB, t=TB)
    xT_s = xT_d.rearrange("b p (s u n) -> u b p s n", s=4, u=2)
    base_s = base_d.rearrange("(b p u h) c -> u b p (h c)", b=NB, u=2, h=2)
    out_s = out.rearrange("(b p u h) c -> u b p (h c)", b=NB, u=2, h=2)
    ys_v = ys_d.rearrange("(j p h) c -> j p (h c)", p=P, h=2)

    ctx = ExitStack()
    with ctx:
        def sem(name):
            return ctx.enter_context(nc.semaphore(name))

        def sem2(name):
            return [sem(name + "_even"), sem(name + "_odd")]

        def sb(stack, name, shape, dt):
            return stack.enter_context(nc.sbuf_tensor(name, shape, dt))

        Wt = sb(ctx, "expert_weights", [P, NCH, 2, CHUNK], f16)
        stage = sb(ctx, "weight_stage", [P, 2, CHUNK], f32)
        xg = sb(ctx, "tile_rows", [P, 2, 2, 2 * C], f16)
        xt = sb(ctx, "tile_rows_T", [P, 2, 4, TILE], f16)
        list_i = sb(ctx, "list_rows", [P, COLS], i32)
        pos_i = sb(ctx, "places", [P, NG * 2], i32)
        wc = sb(ctx, "gate_weights", [P, NG, 2], f32)
        et = sb(ctx, "tile_experts", [1, 3, NT + 1], i32)
        b1s = sb(ctx, "b1_columns", [P, (E + 1) * 8], f32)
        ident = sb(ctx, "ident", [P, P], f16)
        idxc = sb(ctx, "gather_rows", [P, 2, 2], i32)
        idxy = sb(ctx, "gather_places", [P, 2, 2, 4], i32)

        pa = ExitStack()
        xT = sb(pa, "normed_T", [P, 2, 2, 2, SEQ], f16)
        xn = sb(pa, "normed", [P, TB, C], f32)
        xhl = sb(pa, "normed_parts", [P, 2, TB, 2, C], f16)
        rr = sb(pa, "router_hidden", [HID, SEQ], f32)
        qr = sb(pa, "q_relu", [P, 2, SEQ], f32)
        qs = sb(pa, "q_parts", [P, 2, 2, SEQ], f16)
        kr = sb(pa, "k_relu", [P, 2, C], f32)
        ks = sb(pa, "k_parts", [P, 2, TB, C], f16)
        vs = sb(pa, "v_parts", [P, 2, TB, C], f16)
        kvT = sb(pa, "kv_parts", [P, 2, 2, C], f16)
        kvo = sb(pa, "kv_out_parts", [P, 2, 2, C + 4], f16)
        Wrf = sb(pa, "router_w1_f32", [P, 2, HID], f32)
        Wr = sb(pa, "router_w1", [P, 2, 2, HID], f16)
        wr2s = sb(pa, "router_w2", [HID, E], f32)
        br1s = sb(pa, "router_b1", [HID, 1], f32)
        half = sb(pa, "half", [P, 1], f16)
        st = sb(pa, "bn_stats", [P, 2, TB, 6], f32)
        mv = sb(pa, "mean_var_steps", [P, 5, TB], f32)
        mu = sb(pa, "mean", [P, 2, TB], f32)
        ve = sb(pa, "var_eps", [P, 2, TB], f32)
        sd = sb(pa, "std", [P, 2, TB], f32)
        nw = sb(pa, "newton", [P, 4, TB], f32)
        rs = sb(pa, "scaled_rstd", [P, 2, TB], f32)
        zz = sb(pa, "attention_den", [P, 2, TB], f32)
        pa.close()

        hb = sb(ctx, "hidden", [P, 4, 2 * TILE], f32)
        hs = sb(ctx, "hidden_parts", [P, 2, 2, 8, TILE], f16)
        b2b = sb(ctx, "b2_rows", [P, E + 1, C], f32)
        yg = sb(ctx, "expert_rows", [P, 2, 4, C], f32)
        ysb = sb(ctx, "y_rows", [P, 2, 2 * C], f32)
        def gathered(u, late):
            return yg[:, late, :, :] if u == 0 else b2b[:, 1 + 4 * late:5 + 4 * late, :]
        base_o = yg[:, 1, :, :].rearrange("p (q h) c -> p q (h c)", q=2)
        base_c = stage[:, :, 2 * C:4 * C]
        bob = yg[:, 0, 0, :]

        scratch = Wt[:, SCR:NCH, :, :].rearrange("p a s n -> p (a s n)")
        at = [0]

        def carve(shape, dt, parts=P):
            n = 1
            for d in shape:
                n *= d
            words = n * (1 if dt == f16 else 2)
            ap = scratch[0:parts, at[0]:at[0] + words]
            at[0] += words + words % 2
            if dt != f16:
                ap = ap.bitcast(dt)
            if len(shape) == 2:
                ap = ap.rearrange("p (a b) -> p a b", b=shape[1])
            elif len(shape) == 3:
                ap = ap.rearrange("p (a b c) -> p a b c", b=shape[1], c=shape[2])
            return ap

        Wa = carve([2, 2, CHUNK], f16)
        xs = carve([2, TB * C], f32)
        xo = carve([2, TB * C], f32)
        L = carve([NG, E], f32)
        tm = carve([NT * E], f32)
        tb = carve([NG, E], f32)
        M1, M2 = carve([NG, E], f32), carve([NG, E], f32)
        cx = carve([NG + 1, E], f16)
        iota_e, iota_m = carve([NG, E], f32), carve([E, 16], f32)
        br2s = carve([E], f32)
        assert at[0] <= 8 * 2 * CHUNK
        at[0] = 8 * 2 * CHUNK
        oh = carve([4 * TB, P + COLS], f16)
        prow, pcol = carve([NG * 2], f16), carve([NG * 2], f16)
        iota_p, iota_c = carve([P], f16), carve([COLS], f16)
        tok = carve([NG * 2], f16)
        sm = carve([12, NG], f32)
        cum = carve([4, 2 * E], f32)
        iota_j, ej = carve([NT, E], f32, 1), carve([2, NT], f32, 1)
        posf, pint = carve([NG, 2], f32), carve([3, NG * 2], i32)
        before, ones = carve([P], f16), carve([P], f16)
        ranks = carve([NG + 1, E], f32)
        assert at[0] <= (NCH - SCR) * 2 * CHUNK
        ta = tm[:, 0:NG * E].rearrange("p (g e) -> p g e", e=E)
        cmp_m = tm[:, 0:E * 16].rearrange("p (e m) -> p e m", m=16)
        cmp_j = tm[0:1, 0:NT * E].rearrange("p (j e) -> p j e", e=E)

        bank = [ctx.enter_context(nc.psum_tensor(f"bank{i}", [P, 512], f32)) for i in range(8)]
        Q_B = (0, 1)
        KV_B = (2, 3)
        KT_B = 4
        KO_B = (5, 6)
        N_B = 7
        T_B, R_B = Q_B
        UP_B = (2, 3, 5, 6)
        Y_B = (4, 7)

        def bank16(i):
            return bank[i][:, :].bitcast(f16)

        consts_up, small_in, b2_in, bsum_done = sem("consts_up"), sem("small_in"), sem("b2_in"), sem("bsum_done")
        w_in, wo_in, w_hi, w_lo = sem2("weight_loaded"), sem2("opening_weight_loaded"), sem("weight_hi_done"), sem("weight_lo_done")
        wr_hi, wr_lo = sem("router_weight_hi"), sem("router_weight_lo")
        x_in, xo_in, rows_st, base_st = sem2("x_loaded"), sem2("x_again_loaded"), sem2("rows_stored"), sem2("base_stored")
        stats_d, aggr_d, var_d, sd_d = sem("bn_stats_done"), sem("mean_var_step"), sem("var_done"), sem("std_done")
        nw_d, xn_d, xhi_d, xlo_d = sem("newton_step"), sem("normed_done"), sem("normed_hi_done"), sem("normed_lo_done")
        tr_d, xth_d, xtl_d = sem("transposed"), sem("xT_hi_done"), sem("xT_lo_done")
        hid_d, r_d, lg_ps, lg_d = sem("router_hidden_done"), sem("router_relu_done"), sem("logits_product"), sem("logits_done")
        q_ps, qr_d, q_hi, q_lo = sem("q_product"), sem("q_relu_done"), sem("q_hi_done"), sem("q_lo_done")
        kv_ps, kr_d, kv_hi, kv_lo = sem("kv_product"), sem("k_relu_done"), sem("kv_hi_done"), sem("kv_lo_done")
        kt_ps, kt_hi, kt_lo = sem("kvT_product"), sem("kvT_hi_done"), sem("kvT_lo_done")
        ko_ps, ko_hi, ko_lo = sem("kvo_product"), sem("kvo_hi_done"), sem("kvo_lo_done")
        n_ps, n_d, den_d, z_d = sem("num_product"), sem("attended"), sem("den_done"), sem("z_done")
        chain, rexp, dif_d, cx_d = sem("route_step"), sem("route_exp"), sem("route_dif"), sem("chosen_done")
        rank_d, rank_read, route_d = sem("rank_done"), sem("rank_read"), sem("route_done")
        eq_d, oh_d, tab_ps, list_d = sem("columns_compared"), sem("one_hots_done"), sem("list_product"), sem("list_done")
        xT_st, xs_in, xg_in = sem2("xT_stored"), sem2("shared_rows_in"), sem2("tile_rows_in")
        idx_d, tr3_d, xt_d = sem("gather_rows_done"), sem("tile_transposed"), sem("tile_T_done")
        up_ps, h_d, h_hi, h_lo = sem("up_product"), sem("silu_done"), sem("hidden_hi_done"), sem("hidden_lo_done")
        y_ps, y_ev, y_st = sem("down_product"), sem("down_evacuated"), sem2("y_stored")
        bs_in, bs_d = sem2("base_rows_in"), sem("base_added")
        idy_d, yg_in, cb, cb_d = sem2("gather_places_done"), sem2("expert_rows_in_even") + sem2("expert_rows_in_odd"), sem("combine_step"), sem("combined")
        lt_in, lt, lt_d, lt_st = sem2("late_base_in"), sem("late_step"), sem("late_combined"), sem2("late_stored")

        block = ctx.enter_context(nc.Block())

        def chunk_of(c, part):
            return Wt[:, ds(c, 1), part, :].rearrange("p a n -> p (a n)")

        @block.sync
        def _(sp):
            def batch(v, b):
                return v[ds(b, 1)].rearrange("a p n -> (a p) n")

            def shared(v, g, u):
                return v[u, ds(g, 1)].rearrange("a p n -> (a p) n")

            for b in range(2):
                sp.dma_start(xs[:, b, :], x_v[b]).then_inc(x_in[b], 16)
            for dst, src in ((Wrf[:, :, :], wr), (wr2s[:, :], wr2), (br1s[:, :], br1), (b1s[:, :], b1),
                             (br2s, br2.to_broadcast([P, E]))):
                sp.dma_start(dst, src).then_inc(small_in, 16)
            for b in range(2):
                sp.dma_start(xo[:, b, :], x_v[b]).then_inc(xo_in[b], 16)

            def rows_out(b, q):
                sp.wait_ge(xlo_d, b + 1)
                sp.dma_start(batch(rows_v, b), xhl[:, q, :, :, :].rearrange("p t s c -> p (t s c)")).then_inc(rows_st[q], 16)

            def x_load(b, q):
                sp.wait_ge(xn_d, b - 1)
                sp.dma_start(xs[:, q, :], batch(x_v, b)).then_inc(x_in[q], 16)

            def base_out(b, q):
                sp.wait_ge(n_d, b * 4 + 8)
                sp.dma_start(batch(base_v, b), xo[:, q, :]).then_inc(base_st[q], 16)

            def xo_load(b, q, g):
                sp.wait_ge(base_st[q], g * 16 + 16)
                sp.dma_start(xo[:, q, :], batch(x_v, b)).then_inc(xo_in[q], 16)

            def xT_out(b, q):
                sp.wait_ge(xth_d, b + 1)
                sp.wait_ge(xtl_d, b + 1)
                sp.dma_start(batch(xT_d, b), xT[:, q, :, :, :].rearrange("p s c n -> p (s c n)")).then_inc(xT_st[q], 16)

            for b in range(2):
                rows_out(b, b)
                x_load(b + 2, b)
            for b in range(2):
                xT_out(b, b)
            with sp.Fori(0, NB // 2 - 2) as g:
                for q in range(2):
                    b = g * 2 + q
                    rows_out(b + 2, q)
                    x_load(b + 4, q)
                    base_out(b, q)
                    xo_load(b + 2, q, g)
                    xT_out(b + 2, q)
            for b in (NB - 4, NB - 3):
                rows_out(b + 2, b % 2)
                base_out(b, b % 2)
                xo_load(b + 2, b % 2, b // 2)
                xT_out(b + 2, b % 2)
            sp.wait_ge(xT_st[0], 2 * 16)
            for u in range(2):
                sp.dma_start(xt[:, u, :, :], xT_s[u, 0]).then_inc(xs_in[u], 16)
            for b in (NB - 2, NB - 1):
                base_out(b, b % 2)
            def chunks(J):
                for i in range(2):
                    sp.wait_ge(w_lo, J * 2 + (CH_OPEN + 1 + i))
                    sp.dma_start(stage[:, i, :], wts[ds(J * 2 + (CH_OPEN + i), 1)].rearrange("a p n -> (a p) n")).then_inc(wo_in[i], 16)

            def rows_in(f, g, q):
                sp.wait_ge(up_ps, f * 4 - 4)
                sp.dma_start(xt[:, q, :, :], xT_s[q, ds(g, 1)].rearrange("a p s n -> (a p) s n")).then_inc(xs_in[q], 16)

            def opening(g, q, rows_ahead=True, chunks_ahead=True):
                J = g * 2 + q
                if rows_ahead:
                    rows_in(J + 3, g + (3 + q) // 2, 1 - q)
                sp.wait_ge(y_ev, J + 1)
                sp.wait_ge(base_st[0], NB // 2 * 16)
                sp.wait_ge(base_st[1], NB // 2 * 16)
                sp.dma_start(base_o[:, q, :], shared(base_s, g, q)).then_inc(bs_in[q], 16)
                if chunks_ahead:
                    chunks(J + 1)
                sp.wait_ge(y_ev, J + 3)
                sp.dma_start(shared(base_s, g, q), ysb[:, q, :]).then_inc(y_st[q], 16)
            for u in range(2):
                sp.wait_ge(xT_st[u], (NB // 2 + 1) * 16)
            rows_in(2, 1, 0)
            chunks(0)
            with sp.Fori(0, N1 // 2 - 2) as g:
                for q in range(2):
                    opening(g, q)
            opening(N1 // 2 - 2, 0)
            opening(N1 // 2 - 2, 1, rows_ahead=False)
            opening(N1 // 2 - 1, 0, rows_ahead=False)
            opening(N1 // 2 - 1, 1, rows_ahead=False, chunks_ahead=False)

            def y_out(g, q):
                j = g * 2 + q
                sp.wait_ge(y_ev, j + (N1 + 3))
                sp.dma_start(ys_v[ds(j, 1)].rearrange("a p n -> (a p) n"), ysb[:, q, :]).then_inc(y_st[q], 16)
            def closing_rows(g, u):
                sp.wait_ge(up_ps, g * 8 + 4 * (N2 + u - 1))
                sp.dma_start(xt[:, 1 - u, :, :], xT_s[u, ds(g + N1 // 2, 1)].rearrange("a p s n -> (a p) s n")).then_inc(xs_in[1 - u], 16)
            with sp.Fori(0, NT // 2 - 1) as g:
                for q in range(2):
                    y_out(g, q)
            y_out(NT // 2 - 1, 0)
            closing_rows(0, 0)
            y_out(NT // 2 - 1, 1)
            closing_rows(0, 1)
            y_out(NT // 2, 0)

            def base_load(g, u):
                sp.dma_start(base_c[:, 1 - u, :], shared(base_s, g + N1 // 2, u)).then_inc(bs_in[1 - u], 16)

            def late_load(g, u):
                sp.dma_start(stage[:, u, 0:2 * C], shared(base_s, g, u)).then_inc(lt_in[u], 16)
            sp.wait_ge(w_lo, 2 + NCH)
            for u in range(2):
                sp.wait_ge(y_st[u], (N1 // 2 + 1) * 16)
            for u in range(2):
                base_load(0, u)
                late_load(0, u)

            def closing_out(g, u):
                sp.wait_ge(y_ev, g * 2 + (N2 + 3 + u))
                sp.dma_start(shared(out_s, g + N1 // 2, u), ysb[:, 1 - u, :]).then_inc(y_st[1 - u], 16)

            def late_out(g, u):
                sp.wait_ge(lt_d, g * 2 + (u + 3))
                sp.dma_start(shared(out_s, g, u), stage[:, u, 0:2 * C]).then_inc(lt_st[u], 16)
            def closing(g, u, rows_ahead=True):
                closing_out(g, u)
                if rows_ahead:
                    closing_rows(g + 1 + u, 1 - u)
                base_load(g + 1, u)
                late_out(g, u)
                sp.wait_ge(lt_st[u], g * 16 + 16)
                late_load(g + 1, u)
            closing_rows(1, 0)
            with sp.Fori(0, N1 // 2 - 2) as g:
                for u in range(2):
                    closing(g, u)
            closing(N1 // 2 - 2, 0)
            closing(N1 // 2 - 2, 1, rows_ahead=False)
            closing_out(N1 // 2 - 1, 0)
            late_out(N1 // 2 - 1, 0)
            closing_out(N1 // 2 - 1, 1)
            late_out(N1 // 2 - 1, 1)
            sp.wait_ge(y_st[0], ((NALL + 1) // 2 + 1) * 16)
            sp.wait_ge(y_st[1], (NALL // 2 + 1) * 16)
            for u in range(2):
                sp.wait_ge(lt_st[u], N1 // 2 * 16)

        @block.gpsimd
        def _(pool):
            for q in range(2):
                pool.dma_start(stage[:, q, :], wa[q]).then_inc(w_in[q], 16)
            for q in range(2):
                pool.sem_inc(rows_st[q], 16)
                pool.sem_inc(xT_st[q], 16)
                pool.sem_inc(y_st[q], 16)
            pool.sem_inc(n_d, 4)
            pool.sem_inc(tab_ps, 1)
            for s in (tr3_d, y_ev, cb_d, lt_d):
                pool.sem_inc(s, 2)
            pool.sem_inc(h_lo, 4)
            pool.memset(ident[:, :], 0.0)
            pool.memset(before, 1.0)
            pool.memset(ones, 1.0)
            pool.memset(cx[:, NG, :], 0.0)
            pool.memset(cum, 0.0)
            pool.memset(half[:, :], 0.5).then_inc(consts_up, 1)
            pool.wait_ge(consts_up, 1)
            pool.affine_select(out=ident[:, :], in_=ident[:, :], compare_op=ALU.not_equal, fill=1.0,
                               base=0, pattern=[[-1, P]], channel_multiplier=1).then_inc(consts_up, 1)
            pool.affine_select(out=before, in_=before, compare_op=ALU.is_gt, fill=0.0,
                               base=0, pattern=[[1, P]], channel_multiplier=-1)

            def count(dst, pattern, base=0, by_partition=0):
                return pool.iota(dst, pattern=pattern, base=base, channel_multiplier=by_partition,
                                 allow_small_or_imprecise_dtypes=True)
            count(iota_e, [[0, NG], [1, E]])
            count(iota_m, [[0, E], [TILE, 16]])
            count(iota_j, [[1, NT], [0, E]])
            count(iota_p, [[1, P]])
            count(iota_c, [[1, COLS]])
            count(tok, [[SEQ, NB], [1, TB], [0, 2]], base=-(ROWS // 2), by_partition=TB).then_inc(consts_up, 1)
            with pool.Fori(0, CH_OPEN // 2) as g:
                for q in range(2):
                    pool.wait_ge(w_lo, g * 2 + q + 1)
                    pool.dma_start(stage[:, q, :],
                                   wts[ds(g * 2 + q, 1)].rearrange("a p n -> (a p) n")).then_inc(w_in[q], 16)
            pool.wait_ge(n_d, NB * 4 + 4)
            pool.dma_start(b2b[:, :, :].rearrange("p e c -> p (e c)"),
                           b2.to_broadcast([P, (E + 1) * C])).then_inc(b2_in, 16)
            pool.dma_start(bob, bo.to_broadcast([P, C])).then_inc(b2_in, 16)
            pool.wait_ge(list_d, 1)

            def gather(g, q):
                j = g * 2 + q
                pool.wait_ge(tr3_d, j + 1)
                pool.tensor_copy(idxc[:, q, :], list_i[:, ds(j * 2, 2)]).then_inc(idx_d, 1)
                for r in range(2):
                    pool.wait_ge(rows_st[r], (NB // 2 + 1) * 16)
                pool.wait_ge(idx_d, j + 1)
                for h in range(2):
                    pool.indirect_dma_start(
                        out=xg[:, q, h, :], out_offset=None, in_=rows_d[:, :],
                        in_offset=bass.IndirectOffsetOnAxis(ap=idxc[:, q, h:h + 1], axis=0)).then_inc(xg_in[q], 16)
            with pool.Fori(0, NT // 2) as g:
                for q in range(2):
                    gather(g, q)
            gather(NT // 2, 0)

            def expert_rows(g, u, late):
                i = g * 2 + u
                pool.wait_ge(lt_d if late else cb_d, i + 1)
                pool.tensor_copy(idxy[:, u, late, :], pos_i[:, ds(i * 4 + (0 if late else 4 * N1), 4)]).then_inc(idy_d[late], 1)
                for r in range(2):
                    pool.wait_ge(y_st[r], ((N2 + 1 - r) // 2 + 1) * 16)
                pool.wait_ge(idy_d[late], i + 1)
                for k in range(4):
                    pool.indirect_dma_start(
                        out=gathered(u, late)[:, k, :], out_offset=None, in_=ys_d[:, :],
                        in_offset=bass.IndirectOffsetOnAxis(ap=idxy[:, u, late, k:k + 1], axis=0)).then_inc(yg_in[2 * u + late], 16)
            with pool.Fori(0, N1 // 2) as g:
                for u in range(2):
                    expert_rows(g, u, 0)
                    expert_rows(g, u, 1)

        @block.scalar
        def _(act):
            A = nc.scalar.activation

            def split_hi(q, turn, dst, loaded=w_in):
                act.wait_ge(loaded[q], turn * 16 + 16)
                A(dst, stage[:, q, :], ACT.Copy, scale=S_W).then_inc(w_hi, 1)

            def std(b, q):
                act.wait_ge(var_d, b + 1)
                A(sd[:, q, :], ve[:, q, :], ACT.Sqrt).then_inc(sd_d, 1)

            def x_hi(b, q, turn):
                act.wait_ge(xn_d, b + 1)
                act.wait_ge(rows_st[q], turn * 16 + 16)
                A(xhl[:, q, :, 0, :], xn[:, :, :], ACT.Copy).then_inc(xhi_d, 1)

            def xT_hi(b, q, turn):
                act.wait_ge(tr_d, b * 2 + 1)
                act.wait_ge(xT_st[q], turn * 16 + 16)
                A(xT[:, q, 0, :, :].rearrange("p c n -> p (c n)"), bank16(KV_B[0]), ACT.Copy).then_inc(xth_d, 1)

            def router(b):
                act.wait_ge(hid_d, b + 1)
                A(rr[:, :], bank[N_B][0:HID, :], ACT.Relu, bias=br1s[:, 0:1], scale=1.0 / (S_X * S_W)).then_inc(r_d, 1)

            def xT_lo(b, q):
                act.wait_ge(tr_d, b * 2 + 2)
                A(xT[:, q, 1, :, :].rearrange("p c n -> p (c n)"), bank16(KV_B[1]), ACT.Copy).then_inc(xtl_d, 1)

            def q_part(b, h):
                act.wait_ge(q_ps, b * 2 + h + 1)
                A(qr[:, h, :], bank[Q_B[h]][:, :], ACT.Relu, scale=SC).then_inc(qr_d, 1)
                act.wait_ge(qr_d, b * 2 + h + 1)
                A(qs[:, 0, h, :], qr[:, h, :], ACT.Copy, bias=EPS * S_Q).then_inc(q_hi, 1)

            def kv_part(b, t):
                act.wait_ge(kv_ps, b * 4 + t + 1)
                A(kr[:, t % 2, :], bank[KV_B[t % 2]][:, 0:C], ACT.Relu, scale=SC).then_inc(kr_d, 1)
                A(vs[:, 0, t, :], bank[KV_B[t % 2]][:, C:2 * C], ACT.Copy, scale=SC)
                act.wait_ge(kr_d, b * 4 + t + 1)
                A(ks[:, 0, t, :], kr[:, t % 2, :], ACT.Copy, bias=EPS * S_Q).then_inc(kv_hi, 1)

            def kvT_hi(b):
                act.wait_ge(kt_ps, b + 1)
                A(kvT[:, 0, :, :], bank[KT_B][:, :].rearrange("p (h d) -> p h d", h=2), ACT.Copy,
                  scale=S_KV / (S_Q * S_Q)).then_inc(kt_hi, 1)

            def kvo_hi(b):
                act.wait_ge(ko_ps, b + 1)
                for h in range(2):
                    ins = A(kvo[:, 0, h, 0:C + 1], bank[KO_B[h]][:, 0:C + 1], ACT.Copy, scale=1.0 / S_W)
                ins.then_inc(ko_hi, 1)

            def rows_T(j, q):
                act.wait_ge(tr3_d, j + 3)
                A(xt[:, q, :, :].rearrange("p s n -> p (s n)"), bank16(T_B), ACT.Copy).then_inc(xt_d, 1)

            def chunk(b, i):
                split_hi(i % 2, b + (1 + i // 2), chunk_of(b * 2 + i, 0))

            def batch(b, q, g):
                kvT_hi(b)
                router(b + 1)
                std(b + 2, q)
                kv_part(b + 1, 0)
                kvo_hi(b)
                kv_part(b + 1, 1)
                x_hi(b + 2, q, g + 1)
                kv_part(b + 1, 2)
                chunk(b, 0)
                kv_part(b + 1, 3)
                chunk(b, 1)
                q_part(b + 1, 0)
                xT_hi(b + 2, q, g + 1)
                xT_lo(b + 2, q)
                q_part(b + 1, 1)

            act.preload_act_table(ACT.Sqrt)
            std(0, 0)
            act.wait_ge(small_in, 80)
            A(Wr[:, 0, :, :], Wrf[:, :, :], ACT.Copy, scale=S_W).then_inc(wr_hi, 1)
            x_hi(0, 0, 0)
            split_hi(0, 0, Wa[:, 0, 0, :])
            xT_hi(0, 0, 0)
            xT_lo(0, 0)
            split_hi(1, 0, Wa[:, 1, 0, :])
            router(0)
            std(1, 1)
            for t in range(TB):
                kv_part(0, t)
                if t == 1:
                    x_hi(1, 1, 0)
            q_part(0, 0)
            xT_hi(1, 1, 0)
            xT_lo(1, 1)
            q_part(0, 1)
            with act.Fori(0, NB // 2 - 1) as g:
                for q in range(2):
                    batch(g * 2 + q, q, g)
            b = NB - 2
            kvT_hi(b)
            router(b + 1)
            kv_part(b + 1, 0)
            kvo_hi(b)
            kv_part(b + 1, 1)
            chunk(b, 0)
            kv_part(b + 1, 2)
            chunk(b, 1)
            kv_part(b + 1, 3)
            for h in range(2):
                q_part(b + 1, h)
            chunk(b, 2)
            b = NB - 1
            kvT_hi(b)
            chunk(b, 1)
            kvo_hi(b)
            chunk(b, 2)
            act.preload_act_table(ACT.Silu)
            chunk(b, 3)

            def silus(J, q, eb):
                for k in range(5):
                    if k < 4:
                        act.wait_ge(up_ps, J * 4 + k + 1)
                        act.wait_ge(h_lo, J * 4 + k + 1)
                        for i in range(2):
                            ins = A(hb[:, k, i * TILE:(i + 1) * TILE], bank[UP_B[k]][:, i * TILE:(i + 1) * TILE], ACT.Silu,
                                    bias=b1s[:, ds(eb + (2 * k + i), 1)], scale=1.0 / (S_X * S_W))
                        ins.then_inc(h_d, 1)
                    if k > 0:
                        act.wait_ge(h_d, J * 4 + k)
                        A(hs[:, q, 0, 2 * k - 2:2 * k, :].rearrange("p i n -> p (i n)"), hb[:, k - 1, :],
                          ACT.Copy, scale=S_H).then_inc(h_hi, 1)

            def opening(g, q):
                J = g * 2 + q
                silus(J + 1, 1 - q, 0)
                opening_chunks(J)

            def opening_chunks(J):
                for i in range(2):
                    split_hi(i, J, chunk_of(J * 2 + (CH_OPEN + i), 0), wo_in)

            act.wait_ge(n_d, NB * 4 + 4)
            silus(0, 0, 0)
            for i in (4, 5):
                chunk(b, i)
            silus(1, 1, 0)
            act.preload_act_table(ACT.Exp)
            act.wait_ge(dif_d, 1)
            A(tb, tb, ACT.Exp).then_inc(rexp, 1)
            A(sm[:, 5, :], sm[:, 4, :], ACT.Exp).then_inc(rexp, 1)
            act.wait_ge(dif_d, 2)
            A(sm[:, 9, :], sm[:, 8, :], ACT.Exp, scale=0.5).then_inc(rexp, 1)
            act.preload_act_table(ACT.Silu)
            opening_chunks(0)
            silus(2, 0, 0)
            opening_chunks(1)
            with act.Fori(1, N1 // 2 - 1) as g:
                for q in range(2):
                    opening(g, q)
            act.wait_ge(tab_ps, 5)
            opening_chunks(N1 - 2)
            silus(N1 - 1, 1, 0)
            opening_chunks(N1 - 1)
            rows_T(0, 0)
            rows_T(1, 1)
            act.wait_ge(route_d, 1)
            silus(N1, 0, act.value_load(et[0:1, 2, 0:1], min_val=0, max_val=8 * E))
            def expert_tile(j, q):
                silus(j + N1, q, act.value_load(et[0:1, 2, ds(j, 1)], min_val=0, max_val=8 * E))
            with act.Fori(0, NT // 2 - 1) as g:
                for q in range(2):
                    j = g * 2 + (1 + q)
                    expert_tile(j, 1 - q)
                    rows_T(j + 1, q)
            expert_tile(NT - 2, 1)
            rows_T(NT - 1, 0)
            expert_tile(NT - 1, 0)
            with act.Fori(0, N1 // 2) as g:
                for u in range(2):
                    silus(g * 2 + (N2 + u), 1 - u, 0)

        @block.vector
        def _(dve):
            V = nc.vector
            steps = [0]

            def link(ins):
                steps[0] += 1
                ins.then_inc(chain, 1)
                dve.wait_ge(chain, steps[0])

            def split_lo(n, q, hi, lo):
                dve.wait_ge(w_hi, n + 1)
                V.scalar_tensor_tensor(out=lo, in0=stage[:, q, :], scalar=S_W, in1=hi,
                                       op0=ALU.mult, op1=ALU.subtract).then_inc(w_lo, 1)

            def chunk(b, i):
                c = b * 2 + i
                split_lo(c + 2, i % 2, chunk_of(c, 0), chunk_of(c, 1))

            def stats(b, q, turn):
                dve.wait_ge(x_in[q], turn * 16 + 16)
                for t in range(TB):
                    ins = V.bn_stats(st[:, q, t, :], xs[:, q, t * C:(t + 1) * C])
                ins.then_inc(stats_d, 1)

            def variance(b, q):
                dve.wait_ge(stats_d, b + 1)
                m0, v0, m1, v1 = (st[:, q, :, k] for k in (1, 2, 4, 5))
                V.tensor_tensor(mv[:, 0, :], m0, m1, ALU.add)
                V.tensor_tensor(mv[:, 1, :], m0, m1, ALU.subtract)
                V.tensor_tensor(mv[:, 2, :], v0, v1, ALU.add).then_inc(aggr_d, 1)
                dve.wait_ge(aggr_d, b * 2 + 1)
                V.tensor_scalar(mu[:, q, :], mv[:, 0, :], 0.5, None, ALU.mult)
                V.tensor_tensor(mv[:, 3, :], mv[:, 1, :], mv[:, 1, :], ALU.mult)
                V.tensor_scalar(mv[:, 4, :], mv[:, 2, :], 1.0 / C, LN_EPS, ALU.mult, ALU.add).then_inc(aggr_d, 1)
                dve.wait_ge(aggr_d, b * 2 + 2)
                V.scalar_tensor_tensor(out=ve[:, q, :], in0=mv[:, 3, :], scalar=0.25, in1=mv[:, 4, :],
                                       op0=ALU.mult, op1=ALU.add).then_inc(var_d, 1)

            def scale(b, q):
                def step(ins, k):
                    ins.then_inc(nw_d, 1)
                    dve.wait_ge(nw_d, b * 5 + k)
                dve.wait_ge(sd_d, b + 1)
                step(V.reciprocal(nw[:, 0, :], sd[:, q, :]), 1)
                step(V.tensor_tensor(nw[:, 1, :], nw[:, 0, :], nw[:, 0, :], ALU.mult), 2)
                step(V.tensor_tensor(nw[:, 2, :], nw[:, 1, :], ve[:, q, :], ALU.mult), 3)
                step(V.tensor_scalar(nw[:, 3, :], nw[:, 2, :], -0.5 * S_X, 1.5 * S_X, ALU.mult, ALU.add), 4)
                step(V.tensor_tensor(rs[:, q, :], nw[:, 0, :], nw[:, 3, :], ALU.mult), 5)

            def norm(b, q, first=False):
                if not first:
                    dve.wait_ge(xlo_d, b)
                for t in range(TB):
                    ins = V.tensor_scalar(xn[:, t, :], xs[:, q, t * C:(t + 1) * C], mu[:, q, t:t + 1],
                                          rs[:, q, t:t + 1], ALU.subtract, ALU.mult)
                ins.then_inc(xn_d, 1)

            def x_lo(b, q):
                dve.wait_ge(xhi_d, b + 1)
                V.tensor_tensor(xhl[:, q, :, 1, :], xn[:, :, :], xhl[:, q, :, 0, :], ALU.subtract).then_inc(xlo_d, 1)

            def logits(b):
                dve.wait_ge(lg_ps, b + 1)
                V.tensor_tensor(L[:, ds(b * TB, TB), :], bank[N_B][:, 0:TB * E].rearrange("p (t e) -> p t e", e=E),
                                br2s.rearrange("p (a e) -> p a e", a=1).to_broadcast([P, TB, E]), ALU.add).then_inc(lg_d, 1)

            def q_part(b, h):
                dve.wait_ge(q_hi, b * 2 + h + 1)
                V.scalar_tensor_tensor(out=qs[:, 1, h, :], in0=qr[:, h, :], scalar=EPS * S_Q, in1=qs[:, 0, h, :],
                                       op0=ALU.add, op1=ALU.subtract).then_inc(q_lo, 1)

            def kv_part(b, t):
                dve.wait_ge(kv_hi, b * 4 + t + 1)
                V.scalar_tensor_tensor(out=vs[:, 1, t, :], in0=bank[KV_B[t % 2]][:, C:2 * C], scalar=SC, in1=vs[:, 0, t, :],
                                       op0=ALU.mult, op1=ALU.subtract)
                V.scalar_tensor_tensor(out=ks[:, 1, t, :], in0=kr[:, t % 2, :], scalar=EPS * S_Q, in1=ks[:, 0, t, :],
                                       op0=ALU.add, op1=ALU.subtract).then_inc(kv_lo, 1)

            def kvT_lo(b):
                dve.wait_ge(kt_hi, b + 1)
                V.scalar_tensor_tensor(out=kvT[:, 1, :, :], in0=bank[KT_B][:, :].rearrange("p (h d) -> p h d", h=2),
                                       scalar=S_KV / (S_Q * S_Q), in1=kvT[:, 0, :, :],
                                       op0=ALU.mult, op1=ALU.subtract).then_inc(kt_lo, 1)

            def kvo_lo(b):
                dve.wait_ge(ko_hi, b + 1)
                for h in range(2):
                    ins = V.scalar_tensor_tensor(out=kvo[:, 1, h, 0:C + 1], in0=bank[KO_B[h]][:, 0:C + 1], scalar=1.0 / S_W,
                                                 in1=kvo[:, 0, h, 0:C + 1], op0=ALU.mult, op1=ALU.subtract)
                ins.then_inc(ko_lo, 1)

            def attend(b, q, turn, tiles=range(TB)):
                if tiles[0] == 0:
                    dve.wait_ge(xo_in[q], turn * 16 + 16)
                for t in tiles:
                    num = bank[N_B if t % 2 == 0 else KT_B]
                    dve.wait_ge(n_ps, b * 4 + t + 1)
                    V.tensor_scalar_add(zz[:, 0, t:t + 1], num[:, C:C + 1], EPS * S_Q * S_KV).then_inc(den_d, 1)
                    dve.wait_ge(den_d, b * 4 + t + 1)
                    V.reciprocal(zz[:, 1, t:t + 1], zz[:, 0, t:t + 1]).then_inc(z_d, 1)
                    dve.wait_ge(z_d, b * 4 + t + 1)
                    V.scalar_tensor_tensor(out=xo[:, q, t * C:(t + 1) * C], in0=num[:, 0:C], scalar=zz[:, 1, t:t + 1],
                                           in1=xo[:, q, t * C:(t + 1) * C], op0=ALU.mult, op1=ALU.add).then_inc(n_d, 1)

            def batch(b, q, g):
                stats(b + 2, q, g + 1)
                kvT_lo(b)
                variance(b + 2, q)
                scale(b + 2, q)
                norm(b + 2, q)
                kv_part(b + 1, 0)
                kvo_lo(b)
                kv_part(b + 1, 1)
                logits(b + 1)
                x_lo(b + 2, q)
                kv_part(b + 1, 2)
                attend(b, q, g, (0, 1))
                kv_part(b + 1, 3)
                chunk(b, 0)
                attend(b, q, g, (2, 3))
                q_part(b + 1, 0)
                chunk(b, 1)
                q_part(b + 1, 1)

            stats(0, 0, 0)
            variance(0, 0)
            scale(0, 0)
            norm(0, 0, first=True)
            dve.wait_ge(wr_hi, 1)
            V.scalar_tensor_tensor(out=Wr[:, 1, :, :], in0=Wrf[:, :, :], scalar=S_W, in1=Wr[:, 0, :, :],
                                   op0=ALU.mult, op1=ALU.subtract).then_inc(wr_lo, 1)
            x_lo(0, 0)
            split_lo(0, 0, Wa[:, 0, 0, :], Wa[:, 0, 1, :])
            stats(1, 1, 0)
            split_lo(1, 1, Wa[:, 1, 0, :], Wa[:, 1, 1, :])
            variance(1, 1)
            scale(1, 1)
            norm(1, 1)
            for t in range(TB):
                kv_part(0, t)
                if t == 1:
                    logits(0)
                    x_lo(1, 1)
            for h in range(2):
                q_part(0, h)
            with dve.Fori(0, NB // 2 - 1) as g:
                for q in range(2):
                    batch(g * 2 + q, q, g)
            b = NB - 2
            kvT_lo(b)
            kv_part(b + 1, 0)
            kvo_lo(b)
            kv_part(b + 1, 1)
            logits(b + 1)
            kv_part(b + 1, 2)
            attend(b, 0, b // 2, (0, 1))
            chunk(b, 0)
            kv_part(b + 1, 3)
            attend(b, 0, b // 2, (2, 3))
            chunk(b, 1)
            for h in range(2):
                q_part(b + 1, h)
            chunk(b, 2)
            b = NB - 1
            kvT_lo(b)
            chunk(b, 1)
            kvo_lo(b)
            attend(b, 1, b // 2)
            chunk(b, 2)
            chunk(b, 3)

            def over_e(small):
                return small.rearrange("p (g a) -> p g a", a=1).to_broadcast([P, NG, E])
            m1, a1, m2, a2, d2, x2, z, g2, dd, uu, den, tmp = (sm[:, k, :] for k in range(12))

            def choose(best, mask, first_at):
                link(V.tensor_reduce(best, L, AX.X, ALU.max))
                link(V.tensor_tensor(ta, L, over_e(best), ALU.is_equal))
                link(V.scalar_tensor_tensor(out=ta, in0=ta, scalar=-float(E), in1=iota_e, op0=ALU.mult, op1=ALU.add))
                link(V.tensor_reduce(first_at, ta, AX.X, ALU.min))
                link(V.tensor_tensor(mask, ta, over_e(first_at), ALU.is_equal))

            def choices():
                dve.wait_ge(lg_d, NB)
                dve.wait_ge(consts_up, 3)
                choose(m1, M1, a1)
                V.tensor_tensor(tb, L, over_e(m1), ALU.subtract)
                link(V.scalar_tensor_tensor(out=L, in0=M1, scalar=-1e30, in1=L, op0=ALU.mult, op1=ALU.add))
                choose(m2, M2, a2)
                V.tensor_tensor(d2, m2, m1, ALU.subtract).then_inc(dif_d, 1)
                V.tensor_tensor(cx[:, 0:NG, :], M1, M2, ALU.add).then_inc(cx_d, 1)

            def gates():
                dve.wait_ge(rexp, 2)
                link(V.tensor_reduce(tmp, tb, AX.X, ALU.add))
                link(V.reciprocal(z, tmp))
                link(V.tensor_tensor(g2, x2, z, ALU.mult))
                V.tensor_tensor(dd, g2, z, ALU.subtract).then_inc(dif_d, 1)
                dve.wait_ge(rexp, 3)
                link(V.tensor_scalar_add(den, uu, 1.0))
                link(V.reciprocal(wc[:, :, 0], den))
                link(V.tensor_tensor(wc[:, :, 1], uu, wc[:, :, 0], ALU.mult))

            def places():
                link(V.tensor_tensor(cmp_m, ranks[:, NG, :].rearrange("p (e a) -> p e a", a=1).to_broadcast([P, E, 16]),
                                     iota_m, ALU.is_gt))
                link(V.tensor_reduce(cum[:, 0, E:2 * E], cmp_m, AX.X, ALU.add))
                for k, (s, d) in zip((1, 2, 4), ((0, 1), (1, 2), (2, 0))):
                    link(V.tensor_tensor(cum[:, d, E:2 * E], cum[:, s, E:2 * E], cum[:, s, E - k:2 * E - k], ALU.add))
                link(V.tensor_tensor(cmp_j, iota_j,
                                     cum[0:1, 0, E:2 * E].rearrange("p (a e) -> p a e", a=1).to_broadcast([1, NT, E]), ALU.is_ge))
                link(V.tensor_reduce(ej[:, 0, :], cmp_j, AX.X, ALU.add))
                link(V.tensor_scalar_min(ej[:, 1, :], ej[:, 0, :], float(E - 1)))
                for k, by in enumerate((1, CE, 8)):
                    V.tensor_scalar(et[:, k, 0:NT], ej[:, 1, :], float(by), float(by), ALU.mult, ALU.add)
                link(V.scalar_tensor_tensor(out=tb, scalar=float(TILE), in1=ranks[:, 0:NG, :],
                                            in0=cum[:, 0, E - 1:2 * E - 1].rearrange("p (a e) -> p a e", a=1).to_broadcast([P, NG, E]),
                                            op0=ALU.mult, op1=ALU.add))
                V.tensor_tensor(ta, M1, tb, ALU.mult)
                link(V.tensor_tensor(L, M2, tb, ALU.mult))
                V.tensor_reduce(posf[:, :, 0], ta, AX.X, ALU.add)
                link(V.tensor_reduce(posf[:, :, 1], L, AX.X, ALU.add))
                link(V.tensor_copy(pos_i[:, :], posf.rearrange("p g s -> p (g s)")))
                V.tensor_scalar(pint[:, 0, :], pos_i[:, :], 1, P - 1, ALU.logical_shift_right, ALU.bitwise_and)
                V.tensor_scalar(pint[:, 1, :], pos_i[:, :], 8, 1, ALU.logical_shift_right, ALU.logical_shift_left)
                link(V.tensor_scalar(pint[:, 2, :], pos_i[:, :], 1, None, ALU.bitwise_and))
                V.tensor_copy(prow, pint[:, 0, :])
                V.tensor_tensor(pcol, pint[:, 1, :], pint[:, 2, :], ALU.add).then_inc(route_d, 1)

            def ramp(r, n):
                return r.rearrange("p (a n) -> p a n", a=1).to_broadcast([P, 4 * TB, n])

            def pairs(v, m, n):
                return v[:, ds(m * (4 * TB), 4 * TB)].rearrange("p (k a) -> p k a", a=1).to_broadcast([P, 4 * TB, n])

            def columns_equal(m):
                dve.wait_ge(tab_ps, m + 1)
                V.tensor_tensor(oh[:, :, P:], ramp(iota_c, COLS), pairs(pcol, m, COLS), ALU.is_equal).then_inc(eq_d, 1)

            def columns_rows(m):
                dve.wait_ge(eq_d, m + 1)
                V.tensor_tensor(oh[:, :, P:], oh[:, :, P:], pairs(tok, m, COLS), ALU.mult).then_inc(oh_d, 1)

            def partitions_equal(m):
                V.tensor_tensor(oh[:, :, 0:P], ramp(iota_p, P), pairs(prow, m, P), ALU.is_equal).then_inc(oh_d, 1)

            def h_parts(J, q):
                for k in range(4):
                    dve.wait_ge(h_hi, J * 4 + k + 1)
                    V.scalar_tensor_tensor(out=hs[:, q, 1, 2 * k:2 * k + 2, :].rearrange("p i n -> p (i n)"), in0=hb[:, k, :],
                                           scalar=S_H, in1=hs[:, q, 0, 2 * k:2 * k + 2, :].rearrange("p i n -> p (i n)"),
                                           op0=ALU.mult, op1=ALU.subtract).then_inc(h_lo, 1)

            def y_rows(J, q, turn, addend):
                dve.wait_ge(y_ps, J + 1)
                dve.wait_ge(y_st[q], turn * 16 + 16)
                V.scalar_tensor_tensor(out=ysb[:, q, :].rearrange("p (h c) -> p h c", h=2),
                                       in0=bank[Y_B[q]][:, :].rearrange("p (h c) -> p h c", h=2),
                                       scalar=1.0 / (S_H * S_W), in1=addend,
                                       op0=ALU.mult, op1=ALU.add).then_inc(y_ev, 1)

            def chunks(J):
                for i in range(2):
                    c = J * 2 + (CH_OPEN + i)
                    split_lo(c + 2, i, chunk_of(c, 0), chunk_of(c, 1))

            def shared_out(J, q, turn):
                dve.wait_ge(bs_in[q], turn * 16 + 16)
                y_rows(J, q, turn, base_o[:, q, :].rearrange("p (h c) -> p h c", h=2))

            def opening(g, q, m, last=False):
                J = g * 2 + q
                h_parts(J + 1, 1 - q)
                columns_equal(m)
                chunks(J)
                columns_rows(m)
                if last:
                    partitions_equal(m)
                shared_out(J, q, g)
                if not last:
                    partitions_equal(m)

            h_parts(0, 0)
            for i in (4, 5):
                chunk(b, i)
            choices()
            h_parts(1, 1)
            gates()
            shared_out(0, 0, 0)
            chunks(0)
            h_parts(2, 0)
            dve.wait_ge(rank_d, 1)
            V.tensor_copy(ranks.rearrange("p g e -> p (g e)"), bank[R_B][:, 0:(NG + 1) * E]).then_inc(rank_read, 1)
            dve.wait_ge(rank_read, 1)
            chunks(1)
            places()
            dve.wait_ge(route_d, 1)
            shared_out(1, 1, 0)
            opening(1, 0, 0)
            opening(1, 1, 1)
            opening(2, 0, 2)
            opening(2, 1, 3, last=True)
            dve.wait_ge(tab_ps, 5)
            V.tensor_scalar_add(list_i[:, :], bank[R_B][:, 0:COLS], float(ROWS // 2)).then_inc(list_d, 1)
            chunks(N1 - 2)
            h_parts(N1 - 1, 1)
            chunks(N1 - 1)
            shared_out(N1 - 2, 0, N1 // 2 - 1)
            shared_out(N1 - 1, 1, N1 // 2 - 1)
            dve.wait_ge(b2_in, 32)
            V.tensor_tensor(b2b[:, 0, :], b2b[:, 0, :], bob, ALU.add).then_inc(bsum_done, 1)
            dve.wait_ge(bsum_done, 1)
            h_parts(N1, 0)

            def expert_tile(g, q):
                j = g * 2 + q
                h_parts(j + (N1 + 1), 1 - q)
                ev = dve.value_load(et[0:1, 0, ds(j, 1)], min_val=0, max_val=E)
                y_rows(j + N1, q, g + N1 // 2, b2b[:, ds(ev, 1), :].to_broadcast([P, 2, C]))
            with dve.Fori(0, NT // 2) as g:
                for q in range(2):
                    expert_tile(g, q)
            expert_tile(NT // 2, 0)

            def weigh(dst, u, late, f4, s):
                for h in range(2):
                    half_row = dst[:, h * C:(h + 1) * C]
                    ins = V.scalar_tensor_tensor(out=half_row, in0=gathered(u, late)[:, 2 * h + s, :],
                                                 scalar=wc[:, :, :].rearrange("p g s -> p (g s)")[:, ds(f4 + (2 * h + s), 1)],
                                                 in1=half_row, op0=ALU.mult, op1=ALU.add)
                return ins

            def halves(rows):
                return rows.rearrange("p (h c) -> p h c", h=2)
            shared_b2 = b2b[:, 0:1, :].to_broadcast([P, 2, C])

            def late_tile(g, u):
                i = g * 2 + u
                dve.wait_ge(lt_in[u], g * 16 + 16)
                late = stage[:, u, 0:2 * C]
                V.tensor_tensor(halves(late), halves(late), shared_b2, ALU.add).then_inc(lt, 1)
                dve.wait_ge(lt, i * 2 + 1)
                dve.wait_ge(yg_in[2 * u + 1], g * 64 + 64)
                weigh(late, u, 1, i * 4, 0).then_inc(lt, 1)
                dve.wait_ge(lt, i * 2 + 2)
                weigh(late, u, 1, i * 4, 1).then_inc(lt_d, 1)

            def closing_tile(g, u):
                q = 1 - u
                i = g * 2 + u
                dve.wait_ge(bs_in[q], g * 16 + (N1 // 2 + 1) * 16)
                dve.wait_ge(yg_in[2 * u], g * 64 + 64)
                weigh(base_c[:, q, :], u, 0, i * 4 + 4 * N1, 0).then_inc(cb, 1)
                dve.wait_ge(cb, i + 1)
                weigh(base_c[:, q, :], u, 0, i * 4 + 4 * N1, 1).then_inc(cb_d, 1)
                dve.wait_ge(cb_d, i + 3)
                V.tensor_tensor(halves(base_c[:, q, :]), halves(base_c[:, q, :]), shared_b2, ALU.add).then_inc(bs_d, 1)
                dve.wait_ge(bs_d, i + 1)
                y_rows(g * 2 + (N2 + u), q, g + (N2 + u) // 2, halves(base_c[:, q, :]))
            h_parts(N2 + 1, 0)
            closing_tile(0, 0)
            with dve.Fori(0, N1 // 2 - 1) as g:
                late_tile(g, 0)
                h_parts(g * 2 + (N2 + 2), 1)
                closing_tile(g, 1)
                late_tile(g, 1)
                h_parts(g * 2 + (N2 + 3), 0)
                closing_tile(g + 1, 0)
            late_tile(N1 // 2 - 1, 0)
            closing_tile(N1 // 2 - 1, 1)
            late_tile(N1 // 2 - 1, 1)

        @block.tensor
        def _(pe):
            mm = nc.tensor.matmul
            cam = [(c, a, m) for c in range(2) for a, m in THREE]

            def transposes(b, q):
                for s in range(2):
                    pe.wait_ge((xhi_d, xlo_d)[s], b + 1)
                    for c in range(2):
                        for t in range(TB):
                            ins = nc.tensor.transpose(bank16(KV_B[s])[:, c * SEQ + t * P:c * SEQ + (t + 1) * P],
                                                      xhl[:, q, t, s, c * P:(c + 1) * P], ident[:, :])
                    ins.then_inc(tr_d, 1)

            def router_hidden(b, q):
                pe.wait_ge(xth_d, b + 1)
                pe.wait_ge(xtl_d, b + 1)
                for n, (c, a, m) in enumerate(cam):
                    ins = mm(bank[N_B][0:HID, :], Wr[:, a, c, :], xT[:, q, m, c, :], start=(n == 0), stop=(n == 5))
                ins.then_inc(hid_d, 1)

            def router_logits(b):
                pe.wait_ge(r_d, b + 1)
                for t in range(TB):
                    ins = mm(bank[N_B][:, t * E:(t + 1) * E], rr[:, t * P:(t + 1) * P], wr2s[:, :], start=True, stop=True)
                ins.then_inc(lg_ps, 1)

            def q_product(b, q, halves=(0, 1)):
                for h in halves:
                    for n, (c, a, m) in enumerate(cam):
                        ins = mm(bank[Q_B[h]][:, :], Wa[:, c, a, h * P:(h + 1) * P], xT[:, q, m, c, :],
                                 start=(n == 0), stop=(n == 5))
                    ins.then_inc(q_ps, 1)

            def kv_product(b, q, tiles=range(TB)):
                for t in tiles:
                    if t >= 2:
                        pe.wait_ge(kv_lo, b * 4 + t - 1)
                    for n, (c, a, m) in enumerate(cam):
                        ins = mm(bank[KV_B[t % 2]][:, :], xT[:, q, a, c, t * P:(t + 1) * P], Wa[:, c, m, C:3 * C],
                                 start=(n == 0), stop=(n == 5))
                    ins.then_inc(kv_ps, 1)

            def kvT_product(b):
                pe.wait_ge(kv_lo, b * 4 + 4)
                pe.wait_ge(n_d, b * 4 + 4)
                for h in range(2):
                    for n, (t, a, m) in enumerate((t, a, m) for t in range(TB) for a, m in THREE):
                        ins = mm(bank[KT_B][:, h * C:(h + 1) * C], vs[:, a, t, h * P:(h + 1) * P], ks[:, m, t, :],
                                 start=(n == 0), stop=(n == 3 * TB - 1))
                ins.then_inc(kt_ps, 1)
                for h in range(2):
                    for n, (t, a) in enumerate((t, a) for t in range(TB) for a in range(2)):
                        mm(bank[KO_B[h]][:, C:C + 1], ks[:, a, t, h * P:(h + 1) * P], half[:, :],
                           start=(n == 0), stop=(n == 2 * TB - 1))

            def kvo_product(b):
                pe.wait_ge(kt_lo, b + 1)
                for h in range(2):
                    for n, (c, a, m) in enumerate(cam):
                        ins = mm(bank[KO_B[h]][:, 0:C], kvT[:, a, c, h * P:(h + 1) * P], Wa[:, c, m, 3 * C:4 * C],
                                 start=(n == 0), stop=(n == 5))
                ins.then_inc(ko_ps, 1)

            def num_product(b, tiles, logits_read):
                if tiles[0] == 0:
                    pe.wait_ge(ko_lo, b + 1)
                    pe.wait_ge(q_lo, b * 2 + 2)
                    if logits_read:
                        pe.wait_ge(lg_d, b + 2)
                for t in tiles:
                    if t >= 2:
                        pe.wait_ge(n_d, b * 4 + t + 3)
                    for n, (c, a, m) in enumerate(cam):
                        ins = mm(bank[N_B if t % 2 == 0 else KT_B][:, 0:C + 1], qs[:, a, c, t * P:(t + 1) * P],
                                 kvo[:, m, c, 0:C + 1], start=(n == 0), stop=(n == 5))
                    ins.then_inc(n_ps, 1)

            def batch(b, q, norm_ahead):
                kvT_product(b)
                router_hidden(b + 1, 1 - q)
                kv_product(b + 1, 1 - q, (0,))
                kvo_product(b)
                kv_product(b + 1, 1 - q, (1,))
                router_logits(b + 1)
                kv_product(b + 1, 1 - q, (2,))
                num_product(b, (0, 1), True)
                kv_product(b + 1, 1 - q, (3,))
                num_product(b, (2, 3), True)
                q_product(b + 1, 1 - q, (0,))
                if norm_ahead:
                    pe.wait_ge(kv_lo, b * 4 + 8)
                    transposes(b + 2, q)
                q_product(b + 1, 1 - q, (1,))

            pe.wait_ge(consts_up, 2)
            pe.wait_ge(sd_d, 1)
            for _ in range(WARM):
                mm(bank[Q_B[0]][:, 0:P], ident[:, :], ident[:, :], start=True, stop=True)
            transposes(0, 0)
            pe.wait_ge(wr_lo, 1)
            router_hidden(0, 0)
            pe.wait_ge(w_lo, 2)
            kv_product(0, 0, (0, 1))
            router_logits(0)
            kv_product(0, 0, (2, 3))
            q_product(0, 0, (0,))
            pe.wait_ge(kv_lo, TB)
            transposes(1, 1)
            q_product(0, 0, (1,))
            with pe.Fori(0, NB // 2 - 1) as g:
                for q in range(2):
                    batch(g * 2 + q, q, True)
            batch(NB - 2, 0, False)

            def rows_T(j, q, turn):
                pe.wait_ge(xg_in[q], turn * 32 + 32)
                for s in range(4):
                    for h in range(2):
                        ins = nc.tensor.transpose(bank16(T_B)[:, s * TILE + h * P:s * TILE + (h + 1) * P],
                                                  xg[:, q, h, s * P:(s + 1) * P], ident[:, :])
                ins.then_inc(tr3_d, 1)

            def up(J, q, e4, first=False, pairs=range(4)):
                for k in pairs:
                    if not first:
                        pe.wait_ge(h_d, J * 4 + (k - 3))
                    for i in range(2):
                        col = (2 * k + i) * P
                        for n, (c, a, m) in enumerate(cam):
                            ins = mm(bank[UP_B[k]][:, i * TILE:(i + 1) * TILE],
                                     Wt[:, ds(e4 + c, 1), a, col:col + P].rearrange("p a n -> p (a n)"),
                                     xt[:, q, 2 * m + c, :], start=(n == 0), stop=(n == 5))
                    ins.then_inc(up_ps, 1)

            def opening_up(J, q, turn, **kind):
                pe.wait_ge(xs_in[q], turn * 16 + 16)
                up(J, q, 0, **kind)

            def expert_up(j, q):
                e4 = pe.value_load(et[0:1, 1, ds(j, 1)], min_val=0, max_val=CE * E)
                pe.wait_ge(xt_d, j + 1)
                up(j + N1, q, e4)

            def closing_up(J, q, turn):
                pe.wait_ge(xs_in[q], turn * 16 + (N1 // 2 + 1) * 16)
                up(J, q, 0)

            def down(J, q, e4):
                pe.wait_ge(h_lo, J * 4 + 8)
                pe.wait_ge(y_ev, J + 1)
                for h in range(2):
                    for n, (i, a, m) in enumerate((i, a, m) for i in range(8) for a, m in THREE):
                        ins = mm(bank[Y_B[q]][:, h * C:(h + 1) * C], hs[:, q, a, i, h * P:(h + 1) * P],
                                 Wt[:, ds(e4 + (2 + i // 4), 1), m, i % 4 * C:(i % 4 + 1) * C].rearrange("p a n -> p (a n)"),
                                 start=(n == 0), stop=(n == 23))
                ins.then_inc(y_ps, 1)

            b = NB - 1
            kvT_product(b)
            pe.wait_ge(w_lo, 2 + CE)
            opening_up(0, 0, 0, first=True, pairs=(0,))
            kvo_product(b)
            opening_up(0, 0, 0, first=True, pairs=(1,))
            num_product(b, range(TB), False)
            opening_up(0, 0, 0, first=True, pairs=(2, 3))
            opening_up(1, 1, 0)

            def ranks_product():
                pe.wait_ge(cx_d, 1)
                mm(bank[R_B][:, 0:(NG + 1) * E], before, cx.rearrange("p g e -> p (g e)"), start=True, stop=False)
                for t in range(NG):
                    n = NG - t
                    ins = mm(bank[R_B][:, (t + 1) * E:(NG + 1) * E].rearrange("p (n e) -> p n e", e=E), ones,
                             cx[:, t:t + 1, :].to_broadcast([P, n, E]), start=False, stop=(t == NG - 1))
                ins.then_inc(rank_d, 1)

            def list_product(m, first=False, last=False):
                pe.wait_ge(oh_d, m * 2 + 2)
                for k in range(4 * TB):
                    ins = mm(bank[R_B][:, 0:COLS], oh[:, k, 0:P], oh[:, k, P:], start=(first and k == 0),
                             stop=(last and k == 4 * TB - 1))
                ins.then_inc(tab_ps, 1)

            down(0, 0, 0)
            opening_up(2, 0, 1)
            ranks_product()
            down(1, 1, 0)
            opening_up(3, 1, 1)
            down(2, 0, 0)
            opening_up(4, 0, 2)
            down(3, 1, 0)
            list_product(0, first=True)
            with pe.Fori(2, N1 // 2 - 1) as g:
                for q in range(2):
                    opening_up(g * 2 + (q + 1), 1 - q, g + q)
                    down(g * 2 + q, q, 0)
                    list_product(g * 2 + (q - 3))
            opening_up(N1 - 1, 1, N1 // 2 - 1, pairs=(0, 1))
            list_product(3, last=True)
            up(N1 - 1, 1, 0, pairs=(2, 3))
            down(N1 - 2, 0, 0)
            rows_T(0, 0, 0)
            down(N1 - 1, 1, 0)
            pe.wait_ge(xt_d, 1)
            rows_T(1, 1, 0)
            pe.wait_ge(w_lo, 2 + NCH)
            pe.wait_ge(route_d, 1)
            expert_up(0, 0)

            def expert_down(j, q):
                down(j + N1, q, pe.value_load(et[0:1, 1, ds(j, 1)], min_val=0, max_val=CE * E))
            with pe.Fori(0, NT // 2 - 1) as g:
                for q in range(2):
                    j = g * 2 + q
                    expert_up(j + 1, 1 - q)
                    rows_T(j + 2, q, g + 1)
                    expert_down(j, q)
            expert_up(NT - 2, 1)
            rows_T(NT - 1, 0, NT // 2)
            expert_down(NT - 3, 0)
            expert_up(NT - 1, 0)
            expert_down(NT - 2, 1)
            closing_up(N2, 1, 0)
            expert_down(NT - 1, 0)
            with pe.Fori(0, N1 // 2 - 1) as g:
                for u in range(2):
                    J = g * 2 + (N2 + u)
                    closing_up(J + 1, u, g + u)
                    down(J, 1 - u, 0)
            closing_up(NALL - 1, 0, N1 // 2 - 1)
            down(NALL - 2, 1, 0)
            down(NALL - 1, 0, 0)


def kernel(L0_attn_x, L0_attn_W_qkv, L0_attn_W_out, L0_attn_b_out, L0_ffn_Wr1, L0_ffn_br1, L0_ffn_Wr2, L0_ffn_br2,
           L0_ffn_Ws1, L0_ffn_bs1, L0_ffn_Ws2, L0_ffn_bs2, L0_ffn_We1, L0_ffn_be1, L0_ffn_We2, L0_ffn_be2):
    import numpy as np
    import concourse.bacc as bacc
    from concourse.bass_utils import run_bass_kernel_spmd

    a = {k: np.asarray(v) for k, v in dict(locals()).items() if k.startswith("L0_")}
    w1 = np.concatenate([a["L0_ffn_Ws1"][None], a["L0_ffn_We1"]])
    w2 = np.concatenate([a["L0_ffn_Ws2"][None], a["L0_ffn_We2"]])
    w1 = w1.reshape(E + 1, 2, P, I)
    w2 = w2.reshape(E + 1, 2, 4, P, C).transpose(0, 1, 3, 2, 4).reshape(E + 1, 2, P, CHUNK)
    b1 = np.concatenate([a["L0_ffn_bs1"][None], a["L0_ffn_be1"]])
    arrays = {
        "x": a["L0_attn_x"].reshape(ROWS, C),
        "wts": np.concatenate([w1, w2], 1).reshape(NCH, P, CHUNK),
        "wa": np.concatenate([a["L0_attn_W_qkv"].T, a["L0_attn_W_out"].T], 1).reshape(2, P, CHUNK),
        "wr": a["L0_ffn_Wr1"].reshape(2, P, HID).transpose(1, 0, 2),
        "br1": a["L0_ffn_br1"].reshape(HID, 1),
        "wr2": a["L0_ffn_Wr2"],
        "br2": a["L0_ffn_br2"].reshape(1, E),
        "b1": b1.reshape((E + 1) * 8, P).T,
        "b2": np.concatenate([a["L0_ffn_bs2"][None], a["L0_ffn_be2"]]).reshape(1, (E + 1) * C),
        "bo": a["L0_attn_b_out"].reshape(1, C),
    }
    arrays = {f"in_{k}": np.ascontiguousarray(v) for k, v in arrays.items()}
    nc = bacc.Bacc("TRN2", target_bir_lowering=False, num_devices=1)
    args = [nc.dram_tensor(k, v.shape, mybir.dt.from_np(v.dtype), kind="ExternalInput").ap() for k, v in arrays.items()]
    out = nc.dram_tensor("out_dram", (ROWS, C), mybir.dt.float32, kind="ExternalOutput").ap()
    build_program(nc, *args, out)
    r = run_bass_kernel_spmd(nc, [arrays], core_ids=[0])
    return r.results[0]["out_dram"].reshape(a["L0_attn_x"].shape)
```
